# Optimizing a Trainium2 kernel written in Bass

```python
import numpy as np
import jax
import jax.numpy as jnp

def _softmax(x, axis=-1):
    return jax.nn.softmax(x, axis=axis)

def _gelu(x):
    return jax.nn.gelu(x, approximate=True)

def _silu(x):
    return jax.nn.silu(x)

def _sigmoid(x):
    return jax.nn.sigmoid(x)

def _layernorm(x, axis=-1, eps=1e-05):
    m = jnp.mean(x, axis=axis, keepdims=True)
    v = jnp.var(x, axis=axis, keepdims=True)
    return (x - m) / jnp.sqrt(v + eps)

def _scatter_add(tgt, idx, src, axis=0):
    return tgt.at[idx].add(src)

def _segment_sum(src, seg, n):
    return jax.ops.segment_sum(src, seg, n)
kernel_name = 'mk_xattn_seq_d2_seqx_r4_04728d'

def setup_inputs(seed: int=0):
    np.random.seed(seed)
    _w = jnp.asarray

    def _rec_inputs():
        import jax
        import jax.numpy as jnp
        _rk = jax.random.key(seed)
        x = -0.0005146 + 1 * jax.random.normal(jax.random.fold_in(_rk, 1), (16, 256, 512), jnp.float32)
        _lenS = 256 - jax.random.randint(jax.random.fold_in(_rk, 7), (16,), 0, max(1, 256 // 4) + 1, jnp.int32)
        _lenS2 = 256 - jax.random.randint(jax.random.fold_in(_rk, 8), (16,), 0, max(1, 256 // 4) + 1, jnp.int32)
        _ctx_2048P = jax.random.normal(jax.random.fold_in(_rk, 11), (16, 16, 512), jnp.float32)
        _ctx_2048c = jax.random.dirichlet(jax.random.fold_in(_rk, 511), 0.3 * jnp.ones((16,), jnp.float32), (16, 256))
        _ctx_2048t = jnp.einsum('bsk,bkd->bsd', _ctx_2048c, _ctx_2048P)
        _ctx_2048t = _ctx_2048t * jax.lax.rsqrt(jnp.mean(jnp.square(_ctx_2048t)) + 1e-12) * 0.953939
        ctx_2048 = -0.000392918 + 0.999932 * (_ctx_2048t + 0.3 * jax.random.normal(jax.random.fold_in(_rk, 611), (16, 256, 512), jnp.float32))
        _validS = jnp.arange(256)[None, :] < _lenS[:, None]
        _validS2 = jnp.arange(256)[None, :] < _lenS2[:, None]
        _causal = jnp.tril(jnp.ones((256, 256), dtype=bool))
        mask_BxS2_ik0 = jnp.where(jnp.broadcast_to(_validS2[:, :], (16, 256)), 0, 1).astype(jnp.int32)
        mask_BxS2_bf1 = jnp.ones((16, 256), dtype=bool)
        return (x, ctx_2048, mask_BxS2_ik0, mask_BxS2_bf1)
    x, ctx_2048, mask_BxS2_ik0, mask_BxS2_bf1 = _rec_inputs()

    def _L0_xattn_setup():
        import jax, jax.numpy as jnp
        import numpy as np
        B, P, K, H, NH = (4, 512, 64, 512, 16)
        DH = H // NH
        EPS = 1e-06

        def rmsnorm(x, w):
            var = jnp.mean(jnp.square(x), axis=-1, keepdims=True)
            return x * jax.lax.rsqrt(var + EPS) * w
        key = jax.random.key(seed)
        ks = jax.random.split(key, 12)
        s = 0.02
        return {'x': jax.random.normal(ks[0], (B, P, H), jnp.float32), 'latents': jax.random.normal(ks[1], (B, K, H), jnp.float32), 'attention_mask': jax.random.randint(ks[2], (B, P), 0, 2, jnp.int32), 'q_w': s * jax.random.normal(ks[3], (H, H), jnp.float32), 'q_b': jnp.zeros((H,), jnp.float32), 'kv_w': s * jax.random.normal(ks[4], (H, 2 * H), jnp.float32), 'kv_b': jnp.zeros((2 * H,), jnp.float32), 'out_w': s * jax.random.normal(ks[5], (H, H), jnp.float32), 'out_b': jnp.zeros((H,), jnp.float32), 'postnorm_w': jnp.ones((H,), jnp.float32), 'mlp_w1': s * jax.random.normal(ks[6], (H, 4 * H), jnp.float32), 'mlp_b1': jnp.zeros((4 * H,), jnp.float32), 'mlp_w2': s * jax.random.normal(ks[7], (4 * H, H), jnp.float32), 'mlp_b2': jnp.zeros((H,), jnp.float32)}
    _L0_xattn_all = _L0_xattn_setup()
    _L0_xattn_in = {k: v for k, v in _L0_xattn_all.items() if k in ('q_w', 'q_b', 'kv_w', 'kv_b', 'out_w', 'out_b', 'postnorm_w', 'mlp_w1', 'mlp_b1', 'mlp_w2', 'mlp_b2')}
    del _L0_xattn_all

    def _L1_xattn_setup():
        import jax, jax.numpy as jnp
        import numpy as np
        HIDDEN = 512
        HEADS = 16
        HEAD_DIM = HIDDEN // HEADS
        LN_EPS = 1e-05
        GATE_INIT = 0.5

        def _layer_norm(x, gamma, beta):
            mu = jnp.mean(x, axis=-1, keepdims=True)
            var = jnp.mean(jnp.square(x - mu), axis=-1, keepdims=True)
            return (x - mu) * jax.lax.rsqrt(var + LN_EPS) * gamma + beta
        key = jax.random.key(seed)
        ks = jax.random.split(key, 8)
        B, T_TEXT, T_AUDIO = (4, 512, 375)
        s = 0.02
        return {'hidden_states': jax.random.normal(ks[0], (B, T_TEXT, HIDDEN), jnp.float32), 'audio_kv': jax.random.normal(ks[1], (B, T_AUDIO, HIDDEN), jnp.float32), 'audio_attention_mask': jnp.ones((B, T_AUDIO), dtype=bool), 'Wq': jax.random.normal(ks[2], (HIDDEN, HIDDEN), jnp.float32) * s, 'Wk': jax.random.normal(ks[3], (HIDDEN, HIDDEN), jnp.float32) * s, 'Wv': jax.random.normal(ks[4], (HIDDEN, HIDDEN), jnp.float32) * s, 'Wo': jax.random.normal(ks[5], (HIDDEN, HIDDEN), jnp.float32) * s, 'ln_gamma': jnp.ones((HIDDEN,), jnp.float32), 'ln_beta': jnp.zeros((HIDDEN,), jnp.float32), 'gate': jnp.array([GATE_INIT], jnp.float32)}
    _L1_xattn_all = _L1_xattn_setup()
    _L1_xattn_in = {k: v for k, v in _L1_xattn_all.items() if k in ('Wq', 'Wk', 'Wv', 'Wo', 'ln_gamma', 'ln_beta', 'gate')}
    del _L1_xattn_all
    return {'x': x, 'ctx_2048': ctx_2048, 'mask_BxS2_ik0': mask_BxS2_ik0, 'mask_BxS2_bf1': mask_BxS2_bf1, 'L0_xattn_q_w': _L0_xattn_in['q_w'], 'L0_xattn_q_b': _L0_xattn_in['q_b'], 'L0_xattn_kv_w': _L0_xattn_in['kv_w'], 'L0_xattn_kv_b': _L0_xattn_in['kv_b'], 'L0_xattn_out_w': _L0_xattn_in['out_w'], 'L0_xattn_out_b': _L0_xattn_in['out_b'], 'L0_xattn_postnorm_w': _L0_xattn_in['postnorm_w'], 'L0_xattn_mlp_w1': _L0_xattn_in['mlp_w1'], 'L0_xattn_mlp_b1': _L0_xattn_in['mlp_b1'], 'L0_xattn_mlp_w2': _L0_xattn_in['mlp_w2'], 'L0_xattn_mlp_b2': _L0_xattn_in['mlp_b2'], 'L1_xattn_Wq': _L1_xattn_in['Wq'], 'L1_xattn_Wk': _L1_xattn_in['Wk'], 'L1_xattn_Wv': _L1_xattn_in['Wv'], 'L1_xattn_Wo': _L1_xattn_in['Wo'], 'L1_xattn_ln_gamma': _L1_xattn_in['ln_gamma'], 'L1_xattn_ln_beta': _L1_xattn_in['ln_beta'], 'L1_xattn_gate': _L1_xattn_in['gate']}

def reference(x, ctx_2048, mask_BxS2_ik0, mask_BxS2_bf1, L0_xattn_q_w, L0_xattn_q_b, L0_xattn_kv_w, L0_xattn_kv_b, L0_xattn_out_w, L0_xattn_out_b, L0_xattn_postnorm_w, L0_xattn_mlp_w1, L0_xattn_mlp_b1, L0_xattn_mlp_w2, L0_xattn_mlp_b2, L1_xattn_Wq, L1_xattn_Wk, L1_xattn_Wv, L1_xattn_Wo, L1_xattn_ln_gamma, L1_xattn_ln_beta, L1_xattn_gate):
    import jax
    import jax.numpy as jnp

    def _L0_xattn_ref(x, latents, attention_mask, q_w, q_b, kv_w, kv_b, out_w, out_b, postnorm_w, mlp_w1, mlp_b1, mlp_w2, mlp_b2):
        import jax, jax.numpy as jnp
        import numpy as np
        B, P, K, H, NH = (4, 512, 64, 512, 16)
        DH = H // NH
        EPS = 1e-06

        def rmsnorm(x, w):
            var = jnp.mean(jnp.square(x), axis=-1, keepdims=True)
            return x * jax.lax.rsqrt(var + EPS) * w
        b, p, _ = x.shape
        k_len = latents.shape[1]
        residual = latents
        h = jnp.concatenate([x, latents], axis=1)
        q = (latents @ q_w + q_b).reshape(b, k_len, NH, DH)
        kv = (h @ kv_w + kv_b).reshape(b, p + k_len, NH, DH, 2)
        kmat, v = (kv[..., 0], kv[..., 1])
        attn = jnp.einsum('bkhd,bnhd->bhkn', q, kmat) / DH
        full_mask = jnp.concatenate([attention_mask.astype(bool), jnp.ones((b, k_len), bool)], axis=-1)
        attn = jnp.where(full_mask[:, None, None, :], attn, -jnp.inf)
        attn = jax.nn.softmax(attn.astype(jnp.float32), axis=-1).astype(q.dtype)
        attn_out = jnp.einsum('bhkn,bnhd->bkhd', attn, v).reshape(b, k_len, H)
        attn_out = attn_out @ out_w + out_b + residual
        out = rmsnorm(attn_out, postnorm_w)
        out = jax.nn.gelu(out @ mlp_w1 + mlp_b1) @ mlp_w2 + mlp_b2
        return out + residual

    def _L1_xattn_ref(hidden_states, audio_kv, audio_attention_mask, Wq, Wk, Wv, Wo, ln_gamma, ln_beta, gate):
        import jax, jax.numpy as jnp
        import numpy as np
        HIDDEN = 512
        HEADS = 16
        HEAD_DIM = HIDDEN // HEADS
        LN_EPS = 1e-05
        GATE_INIT = 0.5

        def _layer_norm(x, gamma, beta):
            mu = jnp.mean(x, axis=-1, keepdims=True)
            var = jnp.mean(jnp.square(x - mu), axis=-1, keepdims=True)
            return (x - mu) * jax.lax.rsqrt(var + LN_EPS) * gamma + beta
        B, Tt, D = hidden_states.shape
        Ta = audio_kv.shape[1]
        scale = HEAD_DIM ** (-0.5)
        a = _layer_norm(audio_kv, ln_gamma, ln_beta)
        Q = (hidden_states @ Wq.T).reshape(B, Tt, HEADS, HEAD_DIM).transpose(0, 2, 1, 3)
        K = (a @ Wk.T).reshape(B, Ta, HEADS, HEAD_DIM).transpose(0, 2, 1, 3)
        V = (a @ Wv.T).reshape(B, Ta, HEADS, HEAD_DIM).transpose(0, 2, 1, 3)
        scores = jnp.einsum('bhtd,bhsd->bhts', Q, K) * scale
        mask = audio_attention_mask[:, None, None, :]
        scores = jnp.where(mask, scores, jnp.float32(-jnp.inf))
        attn = jax.nn.softmax(scores, axis=-1)
        out = jnp.einsum('bhts,bhsd->bhtd', attn, V)
        out = out.transpose(0, 2, 1, 3).reshape(B, Tt, D)
        out = out @ Wo.T
        return hidden_states + jnp.tanh(gate) * out
    x = _L0_xattn_ref(ctx_2048, x, mask_BxS2_ik0, L0_xattn_q_w, L0_xattn_q_b, L0_xattn_kv_w, L0_xattn_kv_b, L0_xattn_out_w, L0_xattn_out_b, L0_xattn_postnorm_w, L0_xattn_mlp_w1, L0_xattn_mlp_b1, L0_xattn_mlp_w2, L0_xattn_mlp_b2)
    x = _L1_xattn_ref(x, ctx_2048, mask_BxS2_bf1, L1_xattn_Wq, L1_xattn_Wk, L1_xattn_Wv, L1_xattn_Wo, L1_xattn_ln_gamma, L1_xattn_ln_beta, L1_xattn_gate)
    return x

_drawn_inputs = setup_inputs


def setup_inputs(seed=0):
    import zlib

    import numpy as np

    out = dict(_drawn_inputs(seed))
    spreads = {'L0_xattn_q_b': (0.0, 0.8),
     'L0_xattn_kv_b': (0.0, 0.763),
     'L0_xattn_out_b': (0.0, 1.152),
     'L0_xattn_postnorm_w': (1.0, 0.2),
     'L0_xattn_mlp_b1': (0.0, 0.1),
     'L0_xattn_mlp_b2': (0.0, 0.1),
     'L1_xattn_ln_gamma': (1.0, 0.6),
     'L1_xattn_ln_beta': (0.0, 0.8)}
    factors = {'L0_xattn_q_w': 8.0,
     'L0_xattn_kv_w': 8.0,
     'L0_xattn_out_w': 5.05,
     'L1_xattn_Wq': 8.0,
     'L1_xattn_Wk': 8.0}
    for name, (base, spread) in spreads.items():
        noise = np.random.default_rng([zlib.crc32(name.encode()), seed]).standard_normal(out[name].shape)
        drawn = base * np.exp(spread * noise) if base else spread * noise
        out[name] = jnp.asarray(drawn.astype(out[name].dtype))
    for name, factor in factors.items():
        out[name] = (out[name] * factor).astype(out[name].dtype)
    return out
```

```python
import concourse.bass as bass
from concourse import mybir
from contextlib import ExitStack

F32 = mybir.dt.float32
F32R = mybir.dt.float32r
ALU = mybir.AluOpType
ACT = mybir.ActivationFunctionType
AXIS_X = mybir.AxisListType.X

P = 128
B = 16
S = 256
D = 512
FB = D // P
HEADS = 16
DH = D // HEADS
HG = P // DH
QT = S // P
HIDDEN = 4 * D
MB = HIDDEN // P
SPLIT = 3
MASK_ROW = SPLIT * DH
SHIFT_ROW = MASK_ROW + 1
ROWS_MAX = SHIFT_ROW
ROWS_ALL = SHIFT_ROW + 2
MASKED = -1.0e30
RMS_EPS = 1e-6
LN_EPS = 1e-5


def at_least(eng, sem, value):
    if not (isinstance(value, int) and value <= 0):
        eng.wait_ge(sem, value)


def f32(ap):
    return ap.bitcast(F32)


def product(pe, out, left, right, start, stop):
    (left_h, left_l), (right_h, right_l) = left, right
    pe.matmul(out, left_l, right_h, start=start, stop=False)
    pe.matmul(out, left_h, right_l, start=False, stop=False)
    return pe.matmul(out, left_h, right_h, start=False, stop=stop)


def make_identity(pool, ident, done):
    pool.memset(ident[:, :], 0.0).then_inc(done, 1)
    pool.wait_ge(done, 1)
    pool.affine_select(out=ident[:, :], in_=ident[:, :], compare_op=ALU.not_equal, fill=1.0,
                       base=0, pattern=[[-1, P]], channel_multiplier=1).then_inc(done, 1)


def attention_layer(nc, layer, query_src, key_src, mask_src, weights, vectors, residual_src,
                    mask_rows, result):
    first = layer == 0
    KEYS = 2 * S if first else S
    KB = KEYS // P
    KEY_COL = 0 if first else S
    SCALE = 1.0 / DH if first else DH ** -0.5
    HEADS_PER_STEP = 1 if first else 2
    STEPS = HEADS // HEADS_PER_STEP
    PSTEPS = FB * KB
    NT, NK, NQ = FB, FB, FB
    ITEMS = NT + NK + NQ
    STACK_DMAS = 2 * SPLIT * HG + 1
    HALF = HEADS // 2

    x_view = query_src.rearrange("b (t p) d -> b p t d", p=P)
    c_view = key_src.rearrange("b (t p) d -> b p t d", p=P)
    res_view = residual_src.rearrange("b (t p) d -> b p t d", p=P)
    out_view = None if first else result.rearrange("b (t p) d -> b p t d", p=P)

    ctx = ExitStack()
    with ctx:
        def sb(name, shape, dt=F32):
            return ctx.enter_context(nc.sbuf_tensor(f"l{layer}_{name}", shape, dt))

        def pb(name, shape):
            return ctx.enter_context(nc.psum_tensor(f"l{layer}_{name}", shape, F32))

        def sem(name):
            return ctx.enter_context(nc.semaphore(f"l{layer}_{name}"))

        wq = [sb(f"wq_{p}", [P, FB, D], F32R) for p in "hl"]
        wk = [sb(f"wk_{p}", [P, FB, D], F32R) for p in "hl"]
        wv = [sb(f"wv_{p}", [P, FB, D], F32R) for p in "hl"]
        wo = [sb(f"wo_{p}", [P, FB, D], F32R) for p in "hl"]
        tokens = sb("tokens", [P, 2 * QT, D])
        hT = [sb(f"hT_{p}", [P, FB, 2 * S], F32R) for p in "hl"]
        kT = [sb(f"kT_{p}", [P, FB, KEYS], F32R) for p in "hl"]
        qT = [sb(f"qT_{p}", [P, FB, S], F32R) for p in "hl"]
        v = sb("v", [P, KB, D])
        k_stack = sb("k_stack", [ROWS_ALL, HEADS, KEYS], F32R)
        q_stack = sb("q_stack", [ROWS_ALL, HEADS, S], F32R)
        probs = sb("probs", [P, 2, HG * S])
        neg_max = sb("neg_max", [P, QT, HEADS])
        shift = sb("shift", [P, 2, QT, 2 * HALF], F32R)
        shiftT = sb("shiftT", [2 * HALF, 2, S], F32R)
        inv_sum = sb("inv_sum", [P, S])
        o_norm = sb("o_norm", [P, 2, S])
        oT = [sb(f"oT_{p}", [P, FB, S], F32R) for p in "hl"]
        rows = sb("rows", [P, QT, D])
        ident = sb("ident", [P, P])
        ones = sb("ones", [P, DH])
        half_power = sb("half_power", [P, 1])
        eps = sb("eps", [P, QT])
        stat = sb("stat", [P, QT, 8])
        if first:
            nT = sb("nT", [P, FB, S])
            squares = nT[:, :, :].rearrange("p (t a) s -> p t (a s)", t=QT)
            bq, bk, bv, post_w = (sb(n, [P, FB]) for n in ("bq", "bk", "bv", "post_w"))
            bo = sb("bo", [P, D])
            mask_raw = sb("mask_raw", [B, S], mybir.dt.int32)
        else:
            gamma, beta = sb("gamma", [P, FB]), sb("beta", [P, FB])
            aT = sb("aT", [P, 2, S])
            ln_stats = sb("ln_stats", [P, QT, 6])
            gate = sb("gate", [P, 1])
            tanh_gate = sb("tanh_gate", [P, 1])
            any_key, any_inv, gate_b = (sb(n, [P, B]) for n in ("any_key", "any_inv", "gate_b"))
            mask_raw = sb("mask_raw", [B, S], mybir.dt.uint8)
            mask_all = sb("mask_all", [P, B, S], mybir.dt.uint8)
        mask_tile = sb("mask_tile", [B, KEYS])

        item_ps = [pb(f"item_ps{n}", [P, D]) for n in range(2)]
        score_ps = pb("score_ps", [P, 4, 512])
        o_ps = [pb(f"o_ps{n}", [P, D]) for n in range(2)]

        ident_made, const_made = sem("ident_made"), sem("const_made")
        raw_loaded = [sem(f"raw_loaded{n}") for n in range(2)]
        w_turned, w_high, w_low = sem("w_turned"), sem("w_high"), sem("w_low")
        vec_loaded, mask_loaded, mask_made, mask_stored = (
            sem(n) for n in ("vec_loaded", "mask_loaded", "mask_made", "mask_stored"))
        setup_step = sem("setup_step")
        tokens_loaded, item_done, high_done, low_done, part_done = (
            sem(n) for n in ("tokens_loaded", "item_done", "high_done", "low_done", "part_done"))
        v_done, v_copied = sem("v_done"), sem("v_copied")
        ln_step, stats_done, ln_rstd_done = sem("ln_step"), sem("stats_done"), sem("ln_rstd_done")
        stack_loaded = [sem(f"stack_loaded{g}") for g in range(FB)]
        scores_done, max_done, shift_made, shift_turned, shift_copied = (
            sem(n) for n in ("scores_done", "max_done", "shift_made", "shift_turned", "shift_copied"))
        shift_loaded = [sem(f"shift_loaded{h}") for h in range(2)]
        shift_step = sem("shift_step")
        shifted_done, probs_ready, pv_done = sem("shifted_done"), sem("probs_ready"), sem("pv_done")
        inv_done, o_norm_done, o_high_done, o_low_done = (
            sem(n) for n in ("inv_done", "o_norm_done", "o_high_done", "o_low_done"))
        out_done, rows_loaded, rows_biased, rows_done = (
            sem(n) for n in ("out_done", "rows_loaded", "rows_biased", "rows_done"))
        mean_sq_done, rstd_step, rstd_done, norm_done, norm_turned, nT_done, stored = (
            sem(n) for n in ("mean_sq_done", "rstd_step", "rstd_done", "norm_done", "norm_turned",
                             "nT_done", "stored"))

        stage = [probs, tokens]

        def stage_2d(n):
            return stage[n][:, :, :].rearrange("p a b -> p (a b)")

        if first:
            kv_view = weights["kv"].rearrange("(f p) n -> p f n", p=P)
            raw = [kv_view[:, 0:2, :], kv_view[:, 2:4, :],
                   weights["q"].rearrange("(f p) n -> p f n", p=P),
                   weights["o"].rearrange("(f p) n -> p f n", p=P)]
            split_ops = []
            for c in range(2):
                kv = stage_2d(c).rearrange("p (f n two) -> p f n two", f=2, two=2)
                for which, w in ((0, wk), (1, wv)):
                    split_ops.append((c, kv[:, :, :, which], [t[:, 2 * c:2 * c + 2, :] for t in w], 1.0))
            for u, w, scale in ((2, wq, SCALE), (3, wo, 1.0)):
                src = stage_2d(u % 2).rearrange("p (f n) -> p f n", f=FB)
                split_ops.append((u, src, [t[:, :, :] for t in w], scale))
        else:
            raw = [weights[n].rearrange("(f p) n -> p f n", p=P) for n in ("q", "k", "v", "o")]
            split_ops = []
            for u, (w, scale) in enumerate(((wq, SCALE), (wk, 1.0), (wv, 1.0), (wo, 1.0))):
                for f in range(FB):
                    n = FB * u + f
                    split_ops.append((u, item_ps[n % 2][:, :], [t[:, f, :] for t in w], scale))
        last_op_of = [max(n for n, op in enumerate(split_ops) if op[0] == u) for u in range(len(raw))]
        SPLITS = len(split_ops)

        def raw_view(u):
            return stage_2d(u % 2).rearrange("p (f n) -> p f n", f=raw[u].shape[1])

        def shift_after(half):
            return STEPS // 2 * (half + 1) - 1 + 2

        EARLY = max(STEPS, ITEMS)
        SHIFT_AT = [min(shift_after(h), EARLY - 1) for h in range(2)]

        def vectors_to_load():
            def column(vec):
                return vec.rearrange("(f p) -> p f", p=P)
            if first:
                kvb = vectors["kv_b"].rearrange("(f p two) -> p f two", p=P, two=2)
                return [(bq[:, :], column(vectors["q_b"])), (bk[:, :], kvb[:, :, 0]), (bv[:, :], kvb[:, :, 1]),
                        (post_w[:, :], column(vectors["post_w"])),
                        (bo[:, :], vectors["out_b"].partition_broadcast(P))]
            return [(gamma[:, :], column(vectors["gamma"])), (beta[:, :], column(vectors["beta"])),
                    (gate[:, :], vectors["gate"].partition_broadcast(P))]
        VECTORS = 5 if first else 3

        def load_tokens(sp, b):
            sp.dma_start(tokens[:, 0:QT, :], x_view[b]).then_inc(tokens_loaded, 16)
            sp.dma_start(tokens[:, QT:2 * QT, :], c_view[b]).then_inc(tokens_loaded, 16)

        def load_stacks(sp, b, g):
            heads = slice(HG * g, HG * (g + 1))
            for slot, (k_part, q_part) in enumerate(((0, 0), (1, 0), (0, 1))):
                to = slice(DH * slot, DH * (slot + 1))
                for j in range(HG):
                    at = slice(DH * j, DH * (j + 1))
                    sp.dma_start(f32(k_stack[to, HG * g + j, :]), f32(kT[k_part][at, g, :])).then_inc(stack_loaded[g], 16)
                    sp.dma_start(f32(q_stack[to, HG * g + j, :]), f32(qT[q_part][at, g, :])).then_inc(stack_loaded[g], 16)
            sp.dma_start(f32(k_stack[MASK_ROW:MASK_ROW + 1, heads, :]),
                         mask_rows[bass.ds(b, 1), :].rearrange("o (h k) -> o h k", h=1).to_broadcast([1, HG, KEYS])
                         ).then_inc(stack_loaded[g], 16)

        block = ctx.enter_context(nc.Block())

        @block.sync
        def _(sp):
            with nc.allow_non_contiguous_dma(reason="per-feature vectors, once"):
                for dst, src in vectors_to_load():
                    sp.dma_start(dst, src).then_inc(vec_loaded, 16)
            sp.dma_start(mask_raw[:, :], mask_src).then_inc(mask_loaded, 16)
            if not first:
                sp.dma_start(mask_all[:, :, :], mask_src.partition_broadcast(P)).then_inc(mask_loaded, 16)
            for u in range(len(raw)):
                if u >= 2:
                    sp.wait_ge(w_low, last_op_of[u - 2] + 1)
                    if not first:
                        sp.wait_ge(w_turned, last_op_of[u - 2] + 1)
                sp.dma_start(raw_view(u), raw[u]).then_inc(raw_loaded[u % 2], 16)
            sp.wait_ge(mask_made, 1)
            sp.dma_start(mask_rows, mask_tile[:, :]).then_inc(mask_stored, 16)
            sp.wait_ge(w_low, SPLITS)
            load_tokens(sp, 0)
            sp.wait_ge(mask_stored, 16)
            sp.wait_ge(const_made, 5)

            def iteration(p, a):
                if a is not None:
                    at_least(sp, norm_turned if first else stored, a if first else 16 * a)
                    sp.dma_start(rows[:, :, :], res_view[a]).then_inc(rows_loaded, 16)
                if p is not None and not (isinstance(p, int) and p == B - 1):
                    sp.wait_ge(item_done, ITEMS * p + NT)
                    load_tokens(sp, p + 1)
                if a is not None:
                    for half in range(2):
                        sp.wait_ge(shift_copied, 2 * a + half + 1)
                        for part in range(2):
                            sp.dma_start(
                                f32(q_stack[SHIFT_ROW + part:SHIFT_ROW + part + 1,
                                            HALF * half:HALF * (half + 1), :]),
                                f32(shiftT[HALF * part:HALF * (part + 1), half:half + 1, :]),
                            ).then_inc(shift_loaded[half], 16)
                if p is not None:
                    for g in range(FB):
                        if a is None:
                            sp.wait_ge(low_done, ITEMS * p + NT + NK + g + 1)
                        else:
                            sp.wait_ge(shifted_done, PSTEPS * a + KB * (g + 1))
                        load_stacks(sp, p, g)
                if a is not None:
                    if first:
                        sp.wait_ge(nT_done, a + 1)
                        sp.dma_start(result[a], nT[:, :, :]).then_inc(stored, 16)
                    else:
                        sp.wait_ge(rows_done, a + 1)
                        sp.dma_start(out_view[a], rows[:, :, :]).then_inc(stored, 16)

            iteration(0, None)
            with sp.Fori(1, B - 1) as i:
                iteration(i, i - 1)
            iteration(B - 1, B - 2)
            iteration(None, B - 1)
            sp.wait_ge(stored, 16 * B)

        @block.gpsimd
        def _(pool):
            make_identity(pool, ident, ident_made)
            pool.wait_ge(ident_made, 2)
            pool.memset(ones[:, :], 1.0).then_inc(const_made, 1)
            pool.wait_ge(const_made, 1)
            pool.memset(half_power[:, :], -0.5).then_inc(const_made, 1)
            pool.wait_ge(const_made, 2)
            pool.memset(eps[:, :], RMS_EPS if first else LN_EPS).then_inc(const_made, 1)
            pool.wait_ge(const_made, 3)
            pool.memset(f32(k_stack[MASK_ROW:ROWS_ALL, :, :]), 1.0).then_inc(const_made, 1)
            pool.wait_ge(const_made, 4)
            pool.memset(f32(q_stack[MASK_ROW:ROWS_ALL, :, :]), 1.0).then_inc(const_made, 1)
            pool.wait_ge(const_made, 5)

            def ln_rstd(b):
                pool.wait_ge(stats_done, b + 1)
                for t in range(QT):
                    pool.tensor_tensor(stat[:, t, 1:2], stat[:, t, 1:2], eps[:, 0:1], ALU.add).then_inc(rstd_step, 1)
                pool.wait_ge(rstd_step, QT * (b + 1))
                for t in range(QT):
                    n = pool.tensor_tensor(stat[:, t, 2:3], stat[:, t, 1:2], half_power[:, 0:1], ALU.pow)
                n.then_inc(ln_rstd_done, 1)

            def iteration(p, a):
                if first and a is not None:
                    pool.wait_ge(rows_loaded, 16 * (a + 1))
                    for t in range(QT):
                        n = pool.tensor_tensor(rows[:, t, :], rows[:, t, :], bo[:, :], ALU.add)
                    n.then_inc(rows_biased, 1)
                    pool.wait_ge(mean_sq_done, a + 1)
                    pool.tensor_tensor(stat[:, :, 1], stat[:, :, 0], eps[:, :], ALU.add).then_inc(rstd_step, 1)
                    pool.wait_ge(rstd_step, a + 1)
                    for t in range(QT):
                        n = pool.tensor_tensor(stat[:, t, 2:3], stat[:, t, 1:2], half_power[:, 0:1], ALU.pow)
                    n.then_inc(rstd_done, 1)
                if not first and p is not None and not (isinstance(p, int) and p == B - 1):
                    ln_rstd(p + 1)

            if first:
                pool.wait_ge(vec_loaded, 16 * VECTORS)
            else:
                ln_rstd(0)
            iteration(0, None)
            with pool.Fori(1, B - 1) as i:
                iteration(i, i - 1)
            iteration(B - 1, B - 2)
            iteration(None, B - 1)

        @block.scalar
        def _(act):
            for n, (u, src, (high, _low), scale) in enumerate(split_ops):
                if first:
                    act.wait_ge(raw_loaded[u % 2], 16 * (u // 2 + 1))
                else:
                    act.wait_ge(w_turned, n + 1)
                act.activation(high, src, ACT.Copy, scale=scale).then_inc(w_high, 1)
            act.wait_ge(vec_loaded, 16 * VECTORS)
            if first:
                act.wait_ge(setup_step, 1)
            else:
                act.activation(tanh_gate[:, :], gate[:, :], ACT.Tanh).then_inc(setup_step, 1)

            def high(b, k):
                act.wait_ge(item_done, ITEMS * b + k + 1)
                ps, done = item_ps[k % 2], ITEMS * b + k + 1
                if k < NT:
                    at_least(act, v_done, KB * b)
                    if first:
                        n = act.activation(hT[0][:, k, :], ps[:, :], ACT.Copy)
                    else:
                        act.activation(hT[0][:, k, 0:S], ps[:, 0:S], ACT.Copy)
                        n = act.activation(hT[0][:, k, S:2 * S], ps[:, S:2 * S], ACT.Identity,
                                           bias=beta[:, k:k + 1], scale=gamma[:, k:k + 1])
                elif k < NT + NK:
                    g = k - NT
                    at_least(act, stack_loaded[g], 16 * STACK_DMAS * b)
                    if first:
                        n = act.activation(kT[0][:, g, :], ps[:, 0:KEYS], ACT.Identity, bias=bk[:, g:g + 1])
                    else:
                        n = act.activation(kT[0][:, g, :], ps[:, 0:KEYS], ACT.Copy)
                else:
                    g = k - NT - NK
                    if first:
                        n = act.activation(qT[0][:, g, :], ps[:, 0:S], ACT.Identity, bias=bq[:, g:g + 1])
                    else:
                        n = act.activation(qT[0][:, g, :], ps[:, 0:S], ACT.Copy)
                n.then_inc(high_done, 1)

            def copy_shift(a, half):
                act.wait_ge(shift_turned, 2 * a + half + 1)
                at_least(act, shift_loaded[half], 32 * a)
                act.activation(shiftT[:, half, :], o_ps[half][0:2 * HALF, 0:S], ACT.Copy).then_inc(shift_copied, 1)

            def exps(a, s):
                act.wait_ge(shifted_done, PSTEPS * a + s + 1)
                if s >= 2:
                    act.wait_ge(pv_done, PSTEPS * a + s - 1)
                act.activation(probs[:, s % 2, :].rearrange("p (a b) -> p a b", a=2),
                               score_ps[:, 2 * (s % 2):2 * (s % 2) + 2, :], ACT.Exp).then_inc(probs_ready, 1)

            def o_high(a, g):
                act.wait_ge(o_norm_done, FB * a + g + 1)
                at_least(act, out_done, a)
                if first:
                    n = act.activation(oT[0][:, g, :], o_norm[:, g % 2, :], ACT.Identity, bias=bv[:, g:g + 1])
                else:
                    n = act.activation(oT[0][:, g, :], o_norm[:, g % 2, :], ACT.Copy)
                n.then_inc(o_high_done, 1)

            def copy_v(p, t):
                act.wait_ge(v_done, KB * p + t + 1)
                at_least(act, pv_done, PSTEPS * p)
                act.activation(v[:, t, :], score_ps[:, t, :], ACT.Copy).then_inc(v_copied, 1)

            def iteration(p, a):
                for k in range(EARLY):
                    if p is not None and k < ITEMS:
                        high(p, k)
                    for half in range(2):
                        if a is not None and SHIFT_AT[half] == k:
                            copy_shift(a, half)
                if a is not None:
                    for s in range(PSTEPS):
                        exps(a, s)
                        if s >= KB and s % KB == 1:
                            o_high(a, s // KB - 1)
                    o_high(a, FB - 1)
                if p is not None:
                    for t in range(KB):
                        copy_v(p, t)

            iteration(0, None)
            with act.Fori(1, B) as i:
                iteration(i, i - 1)
            iteration(None, B - 1)

        @block.vector
        def _(dve):
            dve.wait_ge(mask_loaded, 16 if first else 32)
            if first:
                dve.memset(mask_tile[:, 0:S], 0.0)
                dve.tensor_scalar(mask_tile[:, S:2 * S], mask_raw[:, :], 0.0, MASKED, ALU.is_equal, ALU.mult
                                  ).then_inc(mask_made, 1)
            else:
                dve.tensor_scalar(mask_tile[:, :], mask_raw[:, :], 0.0, MASKED, ALU.is_equal, ALU.mult
                                  ).then_inc(mask_made, 1)
            for n, (u, src, (high, low), scale) in enumerate(split_ops):
                dve.wait_ge(w_high, n + 1)
                dve.scalar_tensor_tensor(low, src, scale, f32(high), ALU.mult, ALU.subtract).then_inc(w_low, 1)
            dve.wait_ge(vec_loaded, 16 * VECTORS)
            if first:
                dve.tensor_scalar(bq[:, :], bq[:, :], SCALE, None, ALU.mult).then_inc(setup_step, 1)
                dve.wait_ge(setup_step, 1)
            else:
                dve.tensor_reduce(any_key[:, :], mask_all[:, :, :], AXIS_X, ALU.max).then_inc(part_done, 1)
                dve.wait_ge(part_done, 1)
                dve.tensor_scalar(any_key[:, :], any_key[:, :], 0.0, None, ALU.is_gt).then_inc(part_done, 1)
                dve.wait_ge(part_done, 2)
                dve.reciprocal(any_inv[:, :], any_key[:, :]).then_inc(part_done, 1)
                dve.wait_ge(part_done, 3)
                dve.wait_ge(setup_step, 1)
                dve.scalar_tensor_tensor(gate_b[:, :], any_key[:, :], tanh_gate[:, 0:1], any_inv[:, :],
                                         ALU.mult, ALU.mult).then_inc(part_done, 1)
                dve.wait_ge(part_done, 4)

            PARTS0 = 0 if first else 4

            def layer_norm(b):
                dve.wait_ge(tokens_loaded, 32 * (b + 1))
                for t in range(QT):
                    n = dve.bn_stats(ln_stats[:, t, :], tokens[:, QT + t, :])
                n.then_inc(ln_step, 1)
                dve.wait_ge(ln_step, 2 * b + 1)
                dve.memset(stat[:, :, 3:4], 0.0)
                for t in range(QT):
                    n = dve.bn_aggr(stat[:, t, 0:2], ln_stats[:, t, :])
                n.then_inc(stats_done, 1)
                dve.wait_ge(ln_rstd_done, b + 1)
                for t in range(QT):
                    n = dve.tensor_scalar(tokens[:, QT + t, :], tokens[:, QT + t, :], stat[:, t, 0:1],
                                          stat[:, t, 2:3], ALU.subtract, ALU.mult)
                n.then_inc(ln_step, 1)

            def low(b, k):
                dve.wait_ge(high_done, ITEMS * b + k + 1)
                ps = item_ps[k % 2]
                if k < NT:
                    if first:
                        n = dve.tensor_tensor(hT[1][:, k, :], ps[:, :], f32(hT[0][:, k, :]), ALU.subtract)
                    else:
                        dve.tensor_scalar(aT[:, k % 2, :], ps[:, S:2 * S], gamma[:, k:k + 1], beta[:, k:k + 1],
                                          ALU.mult, ALU.add).then_inc(part_done, 1)
                        dve.tensor_tensor(hT[1][:, k, 0:S], ps[:, 0:S], f32(hT[0][:, k, 0:S]), ALU.subtract)
                        dve.wait_ge(part_done, PARTS0 + NT * b + k + 1)
                        n = dve.tensor_tensor(hT[1][:, k, S:2 * S], aT[:, k % 2, :], f32(hT[0][:, k, S:2 * S]),
                                              ALU.subtract)
                elif k < NT + NK:
                    g = k - NT
                    if first:
                        n = dve.scalar_tensor_tensor(kT[1][:, g, :], ps[:, 0:KEYS], bk[:, g:g + 1],
                                                     f32(kT[0][:, g, :]), ALU.add, ALU.subtract)
                    else:
                        n = dve.tensor_tensor(kT[1][:, g, :], ps[:, 0:KEYS], f32(kT[0][:, g, :]), ALU.subtract)
                else:
                    g = k - NT - NK
                    if first:
                        n = dve.scalar_tensor_tensor(qT[1][:, g, :], ps[:, 0:S], bq[:, g:g + 1],
                                                     f32(qT[0][:, g, :]), ALU.add, ALU.subtract)
                    else:
                        n = dve.tensor_tensor(qT[1][:, g, :], ps[:, 0:S], f32(qT[0][:, g, :]), ALU.subtract)
                n.then_inc(low_done, 1)

            def step_max(a, k):
                dve.wait_ge(scores_done, STEPS * a + k + 1)
                banks = score_ps[:, 2 * (k % 2):2 * (k % 2) + 2, :]
                if first:
                    out = neg_max[:, :, k]
                else:
                    banks = banks.rearrange("p h (q n) -> p h q n", q=QT)
                    out = neg_max[:, :, 2 * k:2 * k + 2].rearrange("p q h -> p h q")
                dve.tensor_reduce(out, banks, AXIS_X, ALU.max, negate=True).then_inc(max_done, 1)

            def make_shift(a, half):
                dve.wait_ge(max_done, STEPS * a + STEPS // 2 * (half + 1))
                src = neg_max[:, :, HALF * half:HALF * (half + 1)]
                dve.tensor_copy(shift[:, half, :, 0:HALF], src).then_inc(shift_step, 1)
                dve.wait_ge(shift_step, 2 * a + half + 1)
                dve.tensor_tensor(shift[:, half, :, HALF:2 * HALF], src, f32(shift[:, half, :, 0:HALF]),
                                  ALU.subtract).then_inc(shift_made, 1)

            def normalise(a, g):
                dve.wait_ge(pv_done, PSTEPS * a + KB * (g + 1))
                dve.reciprocal(inv_sum[:, :], o_ps[g % 2][:, S:2 * S]).then_inc(inv_done, 1)
                dve.wait_ge(inv_done, FB * a + g + 1)
                dve.tensor_tensor(o_norm[:, g % 2, :], o_ps[g % 2][:, 0:S], inv_sum[:, :], ALU.mult
                                  ).then_inc(o_norm_done, 1)

            def o_low(a, g):
                dve.wait_ge(o_high_done, FB * a + g + 1)
                if first:
                    n = dve.scalar_tensor_tensor(oT[1][:, g, :], o_norm[:, g % 2, :], bv[:, g:g + 1],
                                                 f32(oT[0][:, g, :]), ALU.add, ALU.subtract)
                else:
                    n = dve.tensor_tensor(oT[1][:, g, :], o_norm[:, g % 2, :], f32(oT[0][:, g, :]), ALU.subtract)
                n.then_inc(o_low_done, 1)

            def finish(a):
                dve.wait_ge(out_done, a + 1)
                if not first:
                    dve.wait_ge(rows_loaded, 16 * (a + 1))
                    for t in range(QT):
                        n = dve.scalar_tensor_tensor(rows[:, t, :], item_ps[t][:, :], gate_b[:, bass.ds(a, 1)],
                                                     rows[:, t, :], ALU.mult, ALU.add)
                    n.then_inc(rows_done, 1)
                    return
                dve.wait_ge(rows_biased, a + 1)
                for t in range(QT):
                    n = dve.tensor_tensor(rows[:, t, :], item_ps[t][:, :], rows[:, t, :], ALU.add)
                n.then_inc(rows_done, 1)
                dve.wait_ge(rows_done, a + 1)
                at_least(dve, stored, 16 * a)
                for t in range(QT):
                    n = dve.tensor_tensor_reduce(out=squares[:, t, :], in0=rows[:, t, :], in1=rows[:, t, :], scale=1.0 / D,
                                                 scalar=0.0, op0=ALU.mult, op1=ALU.add,
                                                 accum_out=stat[:, t, 0:1])
                n.then_inc(mean_sq_done, 1)
                dve.wait_ge(rstd_done, a + 1)
                for t in range(QT):
                    n = dve.tensor_scalar(rows[:, t, :], rows[:, t, :], stat[:, t, 2:3], None, ALU.mult)
                n.then_inc(norm_done, 1)
                dve.wait_ge(norm_turned, a + 1)
                for f in range(FB):
                    n = dve.tensor_scalar(nT[:, f, :], o_ps[f // 2][:, S * (f % 2):S * (f % 2 + 1)],
                                          post_w[:, f:f + 1], None, ALU.mult)
                n.then_inc(nT_done, 1)

            def iteration(p, a):
                for k in range(EARLY + 1):
                    if a is not None and k < STEPS:
                        step_max(a, k)
                        if (k + 1) % (STEPS // 2) == 0:
                            make_shift(a, (k + 1) // (STEPS // 2) - 1)
                    if p is not None and 1 <= k <= ITEMS:
                        low(p, k - 1)
                if not first and p is not None and not (isinstance(p, int) and p == B - 1):
                    layer_norm(p + 1)
                if a is not None:
                    for g in range(FB):
                        normalise(a, g)
                        o_low(a, g)
                    finish(a)

            if not first:
                layer_norm(0)
            iteration(0, None)
            with dve.Fori(1, B - 1) as i:
                iteration(i, i - 1)
            iteration(B - 1, B - 2)
            iteration(None, B - 1)

        @block.tensor
        def _(pe):
            pe.wait_ge(ident_made, 2)
            if not first:
                for n, (u, ps, _parts, _scale) in enumerate(split_ops):
                    if n % FB == 0:
                        pe.wait_ge(raw_loaded[u % 2], 16 * (u // 2 + 1))
                    at_least(pe, w_low, n - 1)
                    f = n % FB
                    for o in range(FB):
                        m = pe.transpose(ps[:, P * o:P * (o + 1)], raw_view(u)[:, o, P * f:P * (f + 1)], ident[:, :])
                    m.then_inc(w_turned, 1)
            pe.wait_ge(w_low, SPLITS)
            pe.wait_ge(const_made, 5)

            def item(b, k):
                ps = item_ps[k % 2]
                if k < 2:
                    at_least(pe, rows_done, b - 1)
                at_least(pe, low_done, ITEMS * b + k - 1)
                if k < NT:
                    if k == 0:
                        if first:
                            pe.wait_ge(tokens_loaded, 32 * (b + 1))
                        else:
                            pe.wait_ge(ln_step, 2 * (b + 1))
                    for t in range(2 * QT):
                        n = pe.transpose(ps[:, P * t:P * (t + 1)], tokens[:, t, P * k:P * (k + 1)], ident[:, :])
                elif k < NT + NK:
                    g = k - NT
                    if g == 0:
                        pe.wait_ge(low_done, ITEMS * b + NT)
                    for f in range(FB):
                        n = product(pe, ps[:, 0:KEYS], [w[:, f, P * g:P * (g + 1)] for w in wk],
                                    [h[:, f, KEY_COL:KEY_COL + KEYS] for h in hT], f == 0, f == FB - 1)
                else:
                    g = k - NT - NK
                    for f in range(FB):
                        n = product(pe, ps[:, 0:S], [w[:, f, P * g:P * (g + 1)] for w in wq],
                                    [h[:, f, 0:S] for h in hT], f == 0, f == FB - 1)
                n.then_inc(item_done, 1)

            def v_item(b, t):
                at_least(pe, probs_ready, PSTEPS * b)
                col = KEY_COL + P * t
                for f in range(FB):
                    n = product(pe, score_ps[:, t, :], [h[:, f, col:col + P] for h in hT],
                                [w[:, f, :] for w in wv], f == 0, f == FB - 1)
                n.then_inc(v_done, 1)

            def scores(a, k):
                if k < 2:
                    pe.wait_ge(v_copied, KB * (a + 1))
                    at_least(pe, probs_ready, PSTEPS * a)
                else:
                    pe.wait_ge(max_done, STEPS * a + k - 1)
                for n in range(2):
                    h = k if first else 2 * k + n
                    if h % HG == 0:
                        pe.wait_ge(stack_loaded[h // HG], 16 * STACK_DMAS * (a + 1))
                    out = score_ps[:, 2 * (k % 2) + n, :]
                    if first:
                        m = pe.matmul(out, q_stack[0:ROWS_MAX, h, P * n:P * (n + 1)], k_stack[0:ROWS_MAX, h, :],
                                      start=True, stop=True)
                    else:
                        for q in range(QT):
                            m = pe.matmul(out[:, S * q:S * (q + 1)], q_stack[0:ROWS_MAX, h, P * q:P * (q + 1)],
                                          k_stack[0:ROWS_MAX, h, :], start=True, stop=True)
                m.then_inc(scores_done, 1)

            def turn_shift(a, half):
                pe.wait_ge(shift_made, 2 * a + half + 1)
                if first:
                    at_least(pe, nT_done, a)
                at_least(pe, o_norm_done, FB * a)
                for q in range(QT):
                    n = pe.transpose(o_ps[half][0:2 * HALF, P * q:P * (q + 1)], f32(shift[:, half, q, :]), ident[:, :])
                n.then_inc(shift_turned, 1)

            def shifted(a, s):
                g, kb = s // KB, s % KB
                if s % (2 * KB) == 0:
                    pe.wait_ge(shift_loaded[s // (2 * KB)], 32 * (a + 1))
                if s < 2:
                    pe.wait_ge(max_done, STEPS * (a + 1) - 1 + s)
                else:
                    pe.wait_ge(probs_ready, PSTEPS * a + s - 1)
                for j in range(HG):
                    h = HG * g + j
                    n = pe.matmul(score_ps[:, 2 * (s % 2) + j // 2, S * (j % 2):S * (j % 2 + 1)],
                                  k_stack[0:ROWS_ALL, h, P * kb:P * (kb + 1)], q_stack[0:ROWS_ALL, h, :],
                                  start=True, stop=True)
                n.then_inc(shifted_done, 1)

            def weigh(a, s):
                g, kb = s // KB, s % KB
                pe.wait_ge(probs_ready, PSTEPS * a + s + 1)
                if kb == 0 and g < 2:
                    pe.wait_ge(shift_copied, 2 * a + g + 1)
                if kb == 0 and g >= 2:
                    pe.wait_ge(o_norm_done, FB * a + g - 1)
                for j in range(HG):
                    h, to = HG * g + j, slice(DH * j, DH * (j + 1))
                    pe.matmul(o_ps[g % 2][to, 0:S], v[:, kb, DH * h:DH * (h + 1)],
                              probs[:, s % 2, S * j:S * (j + 1)], start=(kb == 0), stop=(kb == KB - 1),
                              skip_group_check=True, tile_position=(0, DH * j))
                for j in range(HG):
                    to = slice(DH * j, DH * (j + 1))
                    n = pe.matmul(o_ps[g % 2][to, S:2 * S], ones[:, :], probs[:, s % 2, S * j:S * (j + 1)],
                                  start=False, stop=(kb == KB - 1), skip_group_check=True,
                                  tile_position=(0, DH * j))
                n.then_inc(pv_done, 1)

            def project(a, g):
                pe.wait_ge(o_low_done, FB * a + g + 1)
                for t in range(QT):
                    n = product(pe, item_ps[t][:, :], [o[:, g, P * t:P * (t + 1)] for o in oT],
                                [w[:, g, :] for w in wo], g == 0, g == FB - 1)
                if g == FB - 1:
                    n.then_inc(out_done, 1)

            def turn_norm(a):
                pe.wait_ge(norm_done, a + 1)
                for f in range(FB):
                    for t in range(QT):
                        n = pe.transpose(o_ps[f // 2][:, S * (f % 2) + P * t:S * (f % 2) + P * (t + 1)],
                                         rows[:, t, P * f:P * (f + 1)], ident[:, :])
                n.then_inc(norm_turned, 1)

            def iteration(p, a):
                for k in range(EARLY):
                    if a is not None and k < STEPS:
                        scores(a, k)
                    if p is not None and k < ITEMS:
                        item(p, k)
                    for half in range(2):
                        if a is not None and SHIFT_AT[half] == k:
                            turn_shift(a, half)
                if a is not None:
                    if p is not None:
                        pe.wait_ge(low_done, ITEMS * (p + 1))
                    shifted(a, 0)
                    for s in range(PSTEPS):
                        if s + 1 < PSTEPS:
                            shifted(a, s + 1)
                        weigh(a, s)
                        if s >= KB and s % KB == KB - 1:
                            project(a, s // KB - 1)
                ahead = KB // 2
                if p is not None:
                    for t in range(ahead):
                        v_item(p, t)
                if a is not None:
                    project(a, FB - 1)
                if p is not None:
                    for t in range(ahead, KB):
                        v_item(p, t)
                if first and a is not None:
                    turn_norm(a)

            iteration(0, None)
            with pe.Fori(1, B) as i:
                iteration(i, i - 1)
            iteration(None, B - 1)


def mlp(nc, nT, x, w1, b1, w2, b2, x1):
    CHUNK = 512
    CHUNKS = B * S // CHUNK
    PAIR = CHUNK // S
    TT = CHUNK // P
    LAG = 2
    HBUF = 3

    x_view = x.rearrange("(c e) (t p) d -> c p (e t) d", e=PAIR, p=P)
    x1_view = x1.rearrange("(c e) (t p) d -> c p (e t) d", e=PAIR, p=P)
    nT_view = nT.rearrange("(c e) p f s -> c e p f s", e=PAIR)

    ctx = ExitStack()
    with ctx:
        def sb(name, shape, dt=F32):
            return ctx.enter_context(nc.sbuf_tensor(f"mlp_{name}", shape, dt))

        def sem(name):
            return ctx.enter_context(nc.semaphore(f"mlp_{name}"))

        w1_sb = [sb(f"w1_{p}", [P, FB, HIDDEN], F32R) for p in "hl"]
        w2_sb = [sb(f"w2_{p}", [P, MB, D], F32R) for p in "hl"]
        norm = sb("norm", [P, FB, CHUNK])
        norm_p = [sb(f"norm_{p}", [P, FB, CHUNK], F32R) for p in "hl"]
        hidden = sb("hidden", [P, HBUF, CHUNK])
        hidden_p = [sb(f"hidden_{p}", [P, HBUF, CHUNK], F32R) for p in "hl"]
        rows = sb("rows", [P, TT, D])
        b1_col = sb("b1_col", [P, MB])
        b2_row = sb("b2_row", [P, D])
        hidden_ps = [ctx.enter_context(nc.psum_tensor(f"mlp_hidden_ps{n}", [P, CHUNK], F32)) for n in range(4)]
        sum_ps = [ctx.enter_context(nc.psum_tensor(f"mlp_sum_ps{n}", [P, D], F32)) for n in range(TT)]

        raw_loaded = [sem(f"raw_loaded{n}") for n in range(2)]
        w_high, w_low, vec_loaded = (sem(n) for n in ("w_high", "w_low", "vec_loaded"))
        norm_loaded, norm_high, norm_low = sem("norm_loaded"), sem("norm_high"), sem("norm_low")
        up_done, gelu_done, hidden_low, down_done = (
            sem(n) for n in ("up_done", "gelu_done", "hidden_low", "down_done"))
        rows_loaded, rows_biased, rows_done, stored = (
            sem(n) for n in ("rows_loaded", "rows_biased", "rows_done", "stored"))

        w1_view = w1.rearrange("(f p) n -> p f n", p=P)
        w2_view = w2.rearrange("(m p) n -> p m n", p=P)
        stage = [t[:, :, :].rearrange("p a b -> p (a b)") for t in (norm, rows)]
        units = [(w1_view[:, f, :], [t[:, f, :] for t in w1_sb]) for f in range(FB)]
        units += [(w2_view[:, FB * m:FB * (m + 1), :],
                   [t[:, FB * m:FB * (m + 1), :].rearrange("p m n -> p (m n)") for t in w2_sb]) for m in range(FB)]

        block = ctx.enter_context(nc.Block())

        @block.sync
        def _(sp):
            with nc.allow_non_contiguous_dma(reason="a per-feature vector, once"):
                sp.dma_start(b1_col[:, :], b1.rearrange("(m p) -> p m", p=P)).then_inc(vec_loaded, 16)
            sp.dma_start(b2_row[:, :], b2.partition_broadcast(P)).then_inc(vec_loaded, 16)
            for u, (src, _parts) in enumerate(units):
                if u >= 2:
                    sp.wait_ge(w_low, u - 1)
                dst = stage[u % 2]
                if len(src.shape) == 3:
                    dst = dst.rearrange("p (m n) -> p m n", m=src.shape[1])
                sp.dma_start(dst, src).then_inc(raw_loaded[u % 2], 16)
            sp.wait_ge(w_low, len(units))

            def chunk(c):
                at_least(sp, norm_low, FB * c)
                for e in range(PAIR):
                    sp.dma_start(norm[:, :, S * e:S * (e + 1)], nT_view[c, e]).then_inc(norm_loaded, 16)
                at_least(sp, stored, 16 * c)
                sp.dma_start(rows[:, :, :], x_view[c]).then_inc(rows_loaded, 16)

            def store(c):
                sp.wait_ge(rows_done, TT * (c + 1))
                sp.dma_start(x1_view[c], rows[:, :, :]).then_inc(stored, 16)

            chunk(0)
            with sp.Fori(1, CHUNKS) as c:
                at_least(sp, norm_low, FB * c)
                for e in range(PAIR):
                    sp.dma_start(norm[:, :, S * e:S * (e + 1)], nT_view[c, e]).then_inc(norm_loaded, 16)
                store(c - 1)
                sp.wait_ge(stored, 16 * c)
                sp.dma_start(rows[:, :, :], x_view[c]).then_inc(rows_loaded, 16)
            store(CHUNKS - 1)
            sp.wait_ge(stored, 16 * CHUNKS)

        @block.gpsimd
        def _(pool):
            pool.wait_ge(vec_loaded, 32)
            with pool.Fori(0, CHUNKS) as c:
                pool.wait_ge(rows_loaded, 16 * c + 16)
                for t in range(TT):
                    pool.tensor_tensor(rows[:, t, :], rows[:, t, :], b2_row[:, :], ALU.add).then_inc(rows_biased, 1)

        @block.scalar
        def _(act):
            for u, (_src, (high, _low)) in enumerate(units):
                act.wait_ge(raw_loaded[u % 2], 16 * (u // 2 + 1))
                act.activation(high, stage[u % 2], ACT.Copy).then_inc(w_high, 1)
            act.wait_ge(vec_loaded, 32)
            with act.Fori(0, CHUNKS) as c:
                act.wait_ge(norm_loaded, 16 * PAIR * c + 16 * PAIR)
                act.wait_ge(up_done, MB * c)
                for f in range(FB):
                    act.activation(norm_p[0][:, f, :], norm[:, f, :], ACT.Copy).then_inc(norm_high, 1)
                for m in range(MB):
                    act.wait_ge(up_done, MB * c + m + 1)
                    if m >= HBUF:
                        act.wait_ge(down_done, MB * c + m - HBUF + 1)
                    elif True:
                        act.wait_ge(down_done, MB * c)
                    act.activation(hidden[:, m % HBUF, :], hidden_ps[m % 4][:, :], ACT.Gelu_apprx_tanh,
                                   bias=b1_col[:, m:m + 1])
                    act.activation(hidden_p[0][:, m % HBUF, :], hidden_ps[m % 4][:, :], ACT.Gelu_apprx_tanh,
                                   bias=b1_col[:, m:m + 1]).then_inc(gelu_done, 1)

        @block.vector
        def _(dve):
            for u, (_src, (high, low)) in enumerate(units):
                dve.wait_ge(w_high, u + 1)
                dve.tensor_tensor(low, stage[u % 2], f32(high), ALU.subtract).then_inc(w_low, 1)
            with dve.Fori(0, CHUNKS) as c:
                for f in range(FB):
                    dve.wait_ge(norm_high, FB * c + f + 1)
                    dve.tensor_tensor(norm_p[1][:, f, :], norm[:, f, :], f32(norm_p[0][:, f, :]), ALU.subtract
                                      ).then_inc(norm_low, 1)
                for m in range(MB):
                    dve.wait_ge(gelu_done, MB * c + m + 1)
                    dve.tensor_tensor(hidden_p[1][:, m % HBUF, :], hidden[:, m % HBUF, :],
                                      f32(hidden_p[0][:, m % HBUF, :]), ALU.subtract).then_inc(hidden_low, 1)
                dve.wait_ge(down_done, MB * c + MB)
                dve.wait_ge(rows_biased, TT * c + TT)
                for t in range(TT):
                    dve.tensor_tensor(rows[:, t, :], sum_ps[t][:, :], rows[:, t, :], ALU.add).then_inc(rows_done, 1)

        @block.tensor
        def _(pe):
            pe.wait_ge(w_low, len(units))

            def up(c, m):
                if m >= 4:
                    pe.wait_ge(gelu_done, MB * c + m - 3)
                for f in range(FB):
                    if m == 0:
                        pe.wait_ge(norm_low, FB * c + f + 1)
                    n = product(pe, hidden_ps[m % 4][:, :], [w[:, f, P * m:P * (m + 1)] for w in w1_sb],
                                [t[:, f, :] for t in norm_p], f == 0, f == FB - 1)
                n.then_inc(up_done, 1)

            def down(c, m):
                pe.wait_ge(hidden_low, MB * c + m + 1)
                for t in range(TT):
                    if m == 0:
                        pe.wait_ge(rows_done, TT * c)
                    n = product(pe, sum_ps[t][:, :], [h[:, m % HBUF, P * t:P * (t + 1)] for h in hidden_p],
                                [w[:, m, :] for w in w2_sb], m == 0, m == MB - 1)
                n.then_inc(down_done, 1)

            with pe.Fori(0, CHUNKS) as c:
                for m in range(MB + LAG):
                    if m < MB:
                        up(c, m)
                    if m >= LAG:
                        down(c, m - LAG)


def build(nc, t, out):
    nT = nc.dram_tensor("norm_transposed", [B, P, FB, S], F32).ap()
    x1 = nc.dram_tensor("layer0_result", [B, S, D], F32).ap()
    mask_rows0 = nc.dram_tensor("mask_rows0", [B, 2 * S], F32).ap()
    mask_rows1 = nc.dram_tensor("mask_rows1", [B, S], F32).ap()
    attention_layer(
        nc, 0, t["x"], t["ctx_2048"], t["mask_BxS2_ik0"],
        {"q": t["L0_xattn_q_w"], "kv": t["L0_xattn_kv_w"], "o": t["L0_xattn_out_w"]},
        {"q_b": t["L0_xattn_q_b"], "kv_b": t["L0_xattn_kv_b"], "out_b": t["L0_xattn_out_b"],
         "post_w": t["L0_xattn_postnorm_w"]},
        t["x"], mask_rows0, nT)
    mlp(nc, nT, t["x"], t["L0_xattn_mlp_w1"], t["L0_xattn_mlp_b1"], t["L0_xattn_mlp_w2"],
        t["L0_xattn_mlp_b2"], x1)
    attention_layer(
        nc, 1, x1, t["ctx_2048"], t["mask_BxS2_bf1"],
        {"q": t["L1_xattn_Wq"], "k": t["L1_xattn_Wk"], "v": t["L1_xattn_Wv"], "o": t["L1_xattn_Wo"]},
        {"gamma": t["L1_xattn_ln_gamma"], "beta": t["L1_xattn_ln_beta"], "gate": t["L1_xattn_gate"]},
        x1, mask_rows1, out)


INPUTS = ["x", "ctx_2048", "mask_BxS2_ik0", "mask_BxS2_bf1", "L0_xattn_q_w", "L0_xattn_q_b", "L0_xattn_kv_w",
          "L0_xattn_kv_b", "L0_xattn_out_w", "L0_xattn_out_b", "L0_xattn_postnorm_w", "L0_xattn_mlp_w1",
          "L0_xattn_mlp_b1", "L0_xattn_mlp_w2", "L0_xattn_mlp_b2", "L1_xattn_Wq", "L1_xattn_Wk", "L1_xattn_Wv",
          "L1_xattn_Wo", "L1_xattn_ln_gamma", "L1_xattn_ln_beta", "L1_xattn_gate"]


def kernel(**inputs):
    import numpy as np
    import concourse.bacc as bacc
    from concourse.bass_utils import run_bass_kernel_spmd

    nc = bacc.Bacc("TRN2", target_bir_lowering=False, num_devices=1)
    arrays, tensors = {}, {}
    for name in INPUTS:
        a = np.ascontiguousarray(inputs[name])
        if a.dtype == np.bool_:
            a = a.view(np.uint8)
        arrays[f"in_{name}"] = a
        tensors[name] = nc.dram_tensor(f"in_{name}", a.shape, mybir.dt.from_np(a.dtype), kind="ExternalInput").ap()
    out = nc.dram_tensor("out", [B, S, D], F32, kind="ExternalOutput").ap()
    build(nc, tensors, out)
    done = run_bass_kernel_spmd(nc, [arrays], core_ids=[0])
    return done.results[0]["out"]
```

```python
import concourse.bass as bass
from concourse import mybir
from contextlib import ExitStack

F32 = mybir.dt.float32
F32R = mybir.dt.float32r
ALU = mybir.AluOpType
ACT = mybir.ActivationFunctionType
AXIS_X = mybir.AxisListType.X

P = 128
B = 16
S = 256
D = 512
FB = D // P
HEADS = 16
DH = D // HEADS
HG = P // DH
QT = S // P
HIDDEN = 4 * D
MB = HIDDEN // P
SPLIT = 3
MASK_ROW = SPLIT * DH
SHIFT_ROW = MASK_ROW + 1
ROWS_MAX = SHIFT_ROW
ROWS_ALL = SHIFT_ROW + 2
MASKED = -1.0e30
RMS_EPS = 1e-6
LN_EPS = 1e-5
CHUNK = 512


def at_least(eng, sem, value):
    if not (isinstance(value, int) and value <= 0):
        eng.wait_ge(sem, value)


def f32(ap):
    return ap.bitcast(F32)


def product(pe, out, left, right, start, stop):
    (left_h, left_l), (right_h, right_l) = left, right
    pe.matmul(out, left_l, right_h, start=start, stop=False)
    pe.matmul(out, left_h, right_l, start=False, stop=False)
    return pe.matmul(out, left_h, right_h, start=False, stop=stop)


def make_identity(pool, ident, done):
    pool.memset(ident[:, :], 0.0).then_inc(done, 1)
    pool.wait_ge(done, 1)
    pool.affine_select(out=ident[:, :], in_=ident[:, :], compare_op=ALU.not_equal, fill=1.0,
                       base=0, pattern=[[-1, P]], channel_multiplier=1).then_inc(done, 1)


def attention_layer(nc, layer, query_src, key_src, mask_src, weights, vectors, residual_src,
                    mask_rows, result, room, given, norm_room, ident, source_stored=None, load_ahead=None):
    first = layer == 0
    KEYS = 2 * S if first else S
    KB = KEYS // P
    KEY_COL = 0 if first else S
    SCALE = 1.0 / DH if first else DH ** -0.5
    STEPS = HEADS * (QT if first else 1)
    RING = 4
    PROBS = 3
    PSTEPS = FB * KB
    NT, NK, NQ = FB, FB, (FB // 2 if first else 0)
    ITEMS = NT + NK + NQ
    HALF = HEADS // 2
    HALVES = 2
    GROUPS = FB // HALVES
    WIDTH = S + KEYS
    Q_COLS, K_COLS = slice(0, S), slice(S, WIDTH)
    Q_HIGH, K_LOW = slice(0, S), slice(S, WIDTH)
    Q_LOW, K_HIGH = slice(WIDTH, WIDTH + S), slice(WIDTH + S, 2 * WIDTH)
    STACK_DMAS = HG * 4 + 1
    INV_ROW = 2 * HALF
    SHIFT_ROWS = INV_ROW + HALF
    PLAIN_V = KB - 2
    SLOT = [("share", 0)] + [("v", t) for t in range(PLAIN_V)] + [("item", k) for k in range(ITEMS)]
    SLOTS = len(SLOT)
    STEPS_AT_FIRST = [0, 0, 0, 2, 3, 3, 4, 4, 4, 4, 4, 4, 0] if first else [0, 1, 1, 2, 2, 4, 4, 2, 0]
    STEPS_IN_SLOT = [2, 4, 2, 2, 1, 1, 1, 4, 4, 4, 4, 3, 0] if first else [2, 1, 1, 1, 2, 3, 3, 3, 0]
    AFTER_T = SLOT.index(("item", NT))
    TURN_SLOT = [AFTER_T + (3 if first else 1), SLOTS - 1]
    SPREAD_SLOT = TURN_SLOT[0] + 1
    SQUARE_SLOT, SCALE_SLOT, NORM_SLOT = 1, 3, AFTER_T + 1
    assert max(STEPS_IN_SLOT + STEPS_AT_FIRST) <= RING
    assert len(STEPS_IN_SLOT) == SLOTS and sum(STEPS_IN_SLOT) == STEPS
    assert len(STEPS_AT_FIRST) == SLOTS and sum(STEPS_AT_FIRST) == STEPS

    x_view = query_src.rearrange("b (t p) d -> b p t d", p=P)
    c_view = key_src.rearrange("b (t p) d -> b p t d", p=P)
    res_view = residual_src.rearrange("b (t p) d -> b p t d", p=P)
    out_view = None if first else result.rearrange("b (t p) d -> b p t d", p=P)

    ctx = ExitStack()
    with ctx:
        def sb(name, shape, dt=F32):
            return ctx.enter_context(nc.sbuf_tensor(f"l{layer}_{name}", shape, dt))

        def pb(name, shape):
            return ctx.enter_context(nc.psum_tensor(f"l{layer}_{name}", shape, F32))

        def sem(name):
            return given[name] if name in given else ctx.enter_context(nc.semaphore(f"l{layer}_{name}"))

        wq = [sb(f"wq_{p}", [P, FB, D], F32R) for p in "hl"]
        wk = [sb(f"wk_{p}", [P, FB, D], F32R) for p in "hl"]
        wv = [sb(f"wv_{p}", [P, FB, D], F32R) for p in "hl"]
        wo = [sb(f"wo_{p}", [P, FB, D], F32R) for p in "hl"]
        tokens = (sb("tokens", [P, 2 * QT, D])[:, :, :] if first
                  else room[:, 1, :].rearrange("p (t d) -> p t d", t=2 * QT))
        hT = [sb(f"hT_{p}", [P, FB, 2 * S], F32R) for p in "hl"]
        qk = (room[:, :, :].rearrange("p a b -> p (a b)").rearrange("p (g w) -> p g w", g=FB).bitcast(F32R) if first
              else sb("qk", [P, FB, 2 * WIDTH], F32R)[:, :, :])
        v = sb("v", [P, KB, D])
        stack = sb("stack", [ROWS_ALL, HEADS, WIDTH], F32R)
        probs = sb("probs", [P, PROBS, HG * S])
        neg_max = sb("neg_max", [P, QT, HEADS])
        row_sum = sb("row_sum", [P, QT, HEADS])
        shift = sb("shift", [P, HALVES, QT, SHIFT_ROWS])
        shiftT = sb("shiftT", [SHIFT_ROWS, HALVES, S])
        inv_sum = norm_room[:, :, :]
        spread = sb("spread", [SHIFT_ROWS, GROUPS, P])
        o_norm = sb("o_norm", [P, 2, S])
        oT = [sb(f"oT_{p}", [P, FB, S], F32R) for p in "hl"]
        rows = sb("rows", [P, QT, D])
        half_power = sb("half_power", [P, 1])
        eps = sb("eps", [P, QT])
        stat = sb("stat", [P, QT, 8])
        if first:
            nT = inv_sum
            squares = nT[:, :, :].rearrange("p (t a) s -> p t (a s)", t=QT)
            bq, bk, bv, post_w = (sb(n, [P, FB]) for n in ("bq", "bk", "bv", "post_w"))
            bo = sb("bo", [P, D])
            mask_raw = probs[0:B, PROBS - 1, 0:S].bitcast(mybir.dt.int32)
            mask_tile = probs[0:B, PROBS - 1, S:S + KEYS]
        else:
            gamma, beta = sb("gamma", [P, D]), sb("beta", [P, D])
            ln_stats = sb("ln_stats", [P, QT, 6])
            gate = sb("gate", [P, 1])
            tanh_gate = sb("tanh_gate", [P, 1])
            any_key, any_inv, gate_b = (sb(n, [P, B]) for n in ("any_key", "any_inv", "gate_b"))
            mask_raw = probs[0:B, 0, :].bitcast(mybir.dt.uint8)[:, 0:S]
            mask_tile = probs[0:B, 1, 0:KEYS]
            mask_all = probs[:, PROBS - 1, :].bitcast(mybir.dt.uint8).rearrange("p (b s) -> p b s", b=B)

        item_ps = [pb(f"item_ps{n}", [P, D]) for n in range(2)]
        score_ps = pb("score_ps", [P, 4, 512])
        o_ps = [pb(f"o_ps{n}", [P, D]) for n in range(2)]

        ident_made, const_made = sem("ident_made"), sem("const_made")
        raw_loaded = [sem(f"raw_loaded{n}") for n in range(2)]
        w_turned, w_high, w_low = sem("w_turned"), sem("w_high"), sem("w_low")
        vec_loaded, mask_loaded, mask_made, mask_stored = (
            sem(n) for n in ("vec_loaded", "mask_loaded", "mask_made", "mask_stored"))
        setup_step = sem("setup_step")
        tokens_loaded, item_done, high_done, low_done, part_done = (
            sem(n) for n in ("tokens_loaded", "item_done", "high_done", "low_done", "part_done"))
        v_shared, v_done, v_copied = sem("v_shared"), sem("v_done"), sem("v_copied")
        ln_step, stats_done, ln_rstd_done, ln_scaled, ln_done = (
            sem(n) for n in ("ln_step", "stats_done", "ln_rstd_done", "ln_scaled", "ln_done"))
        stack_loaded = [sem(f"stack_loaded{h}") for h in range(HALVES)]
        scores_done, max_done, sum_done, shift_made, shift_turned, shift_copied = (
            sem(n) for n in ("scores_done", "max_done", "sum_done", "shift_made", "shift_turned", "shift_copied"))
        shift_loaded = [sem(f"shift_loaded{h}") for h in range(2)]
        shift_step, spread_done, inv_copied = sem("shift_step"), sem("spread_done"), sem("inv_copied")
        shifted_done, probs_ready, pv_done = sem("shifted_done"), sem("probs_ready"), sem("pv_done")
        o_norm_done, o_high_done, o_low_done = (
            sem(n) for n in ("o_norm_done", "o_high_done", "o_low_done"))
        out_done, rows_loaded, rows_biased, rows_done = (
            sem(n) for n in ("out_done", "rows_loaded", "rows_biased", "rows_done"))
        mean_sq_done, rstd_step, rstd_done, norm_done, norm_turned, nT_done, stored = (
            sem(n) for n in ("mean_sq_done", "rstd_step", "rstd_done", "norm_done", "norm_turned",
                             "nT_done", "stored"))

        stage = ([probs[:, 0:2, :].rearrange("p a b -> p (a b)"), v[:, :, :].rearrange("p a b -> p (a b)")] if first
                 else [room[:, 0, :], room[:, 2, :]])

        if first:
            kv_view = weights["kv"].rearrange("(f p) n -> p f n", p=P)
            raw = [kv_view[:, 0:2, :], kv_view[:, 2:4, :],
                   weights["o"].rearrange("(f p) n -> p f n", p=P),
                   weights["q"].rearrange("(f p) n -> p f n", p=P)]
            split_ops = []
            for which, w in ((0, wk), (1, wv)):
                for c in range(2):
                    kv = stage[c].rearrange("p (f n two) -> p f n two", f=2, two=2)
                    split_ops.append((c, kv[:, :, :, which], [t[:, 2 * c:2 * c + 2, :] for t in w], 1.0))
            for u, w, scale in ((3, wq, SCALE), (2, wo, 1.0)):
                src = stage[u % 2].rearrange("p (f n) -> p f n", f=FB)
                split_ops.append((u, src, [t[:, :, :] for t in w], scale))
        else:
            raw = [weights[n].rearrange("(f p) n -> p f n", p=P) for n in ("q", "k", "v", "o")]
            split_ops = []
            for u, (w, scale) in enumerate(((wq, SCALE), (wk, 1.0), (wv, 1.0), (wo, 1.0))):
                for f in range(FB):
                    n = FB * u + f
                    split_ops.append((u, score_ps[:, n % RING, :], [t[:, f, :] for t in w], scale))
        last_op_of = [max(n for n, op in enumerate(split_ops) if op[0] == u) for u in range(len(raw))]
        SPLITS = len(split_ops)
        T_ITEMS = [("item", k) for k in range(NT)]
        K_ITEMS = [("item", k) for k in range(NT, NT + NK)]
        Q_ITEMS = [("item", k) for k in range(NT + NK, ITEMS)]
        if first:
            SPLITS_OF_K, SPLITS_OF_Q, SPLITS_OF_V = 2, 5, 5
            FIRST = (T_ITEMS + [("split", n) for n in range(4)] + K_ITEMS[:2] + [("split", 4)] + K_ITEMS[2:] + Q_ITEMS
                     + [("split", 5)])
        else:
            SPLITS_OF_K = SPLITS_OF_Q = 2 * FB
            SPLITS_OF_V = 3 * FB
            FIRST = ([("split", n) for n in range(2 * FB)] + T_ITEMS + K_ITEMS
                     + [("split", n) for n in range(2 * FB, SPLITS)])

        def raw_view(u):
            return stage[u % 2].rearrange("p (f n) -> p f n", f=raw[u].shape[1])

        def steps_of(slot, a):
            counts = STEPS_AT_FIRST if isinstance(a, int) and a == 0 else STEPS_IN_SLOT
            return range(sum(counts[:slot]), sum(counts[:slot + 1]))

        def v_bank(t):
            return item_ps[t][:, :] if t < PLAIN_V else o_ps[t - PLAIN_V][:, :]

        def sums_later(slot):
            kind, n = SLOT[slot]
            return kind == "item" and n < NT

        def kind_of(slot, p, a):
            if not 0 <= slot < SLOTS:
                return None, None
            kind, n = SLOT[slot]
            return (kind, n) if (p if kind == "item" else a) is not None else (None, n)

        def vectors_to_load():
            def column(vec):
                return vec.rearrange("(f p) -> p f", p=P)
            if first:
                kvb = vectors["kv_b"].rearrange("(f p two) -> p f two", p=P, two=2)
                return [(bq[:, :], column(vectors["q_b"])), (bk[:, :], kvb[:, :, 0]), (bv[:, :], kvb[:, :, 1]),
                        (post_w[:, :], column(vectors["post_w"])),
                        (bo[:, :], vectors["out_b"].partition_broadcast(P))]
            return [(gamma[:, :], vectors["gamma"].partition_broadcast(P)), (beta[:, :], vectors["beta"].partition_broadcast(P)),
                    (gate[:, :], vectors["gate"].partition_broadcast(P))]
        VECTORS = 5 if first else 3
        CONSTS = 5

        def load_tokens(sp, b):
            sp.dma_start(tokens[:, 0:QT, :], x_view[b]).then_inc(tokens_loaded, 16)
            sp.dma_start(tokens[:, QT:2 * QT, :], c_view[b]).then_inc(tokens_loaded, 16)

        def load_stacks(sp, b, half):
            def move(slot, j, to_cols, src):
                heads = slice(HALF * half + j, HALF * (half + 1), HG)
                sp.dma_start(f32(stack[DH * slot:DH * (slot + 1), heads, to_cols]), f32(src)
                             ).then_inc(stack_loaded[half], 16)
            for j in range(HG):
                src = qk[DH * j:DH * (j + 1), GROUPS * half:GROUPS * (half + 1), :]
                move(0, j, Q_COLS, src[:, :, Q_HIGH])
                move(0, j, K_COLS, src[:, :, K_HIGH])
                move(1, j, slice(0, WIDTH), src[:, :, 0:WIDTH])
                move(2, j, slice(0, WIDTH), src[:, :, WIDTH:2 * WIDTH])
            sp.dma_start(f32(stack[MASK_ROW:MASK_ROW + 1, HALF * half:HALF * (half + 1), K_COLS]),
                         mask_rows[bass.ds(b, 1), :].rearrange("o (h k) -> o h k", h=1).to_broadcast([1, HALF, KEYS])
                         ).then_inc(stack_loaded[half], 16)

        block = ctx.enter_context(nc.Block())

        @block.sync
        def _(sp):
            def load_raw(u):
                sp.dma_start(raw_view(u), raw[u]).then_inc(raw_loaded[u % 2], 16)

            if first:
                load_tokens(sp, 0)
                sp.wait_ge(tokens_loaded, 32)
                load_raw(0)
                load_raw(1)
            with nc.allow_non_contiguous_dma(reason="per-feature vectors, once"):
                for dst, src in vectors_to_load():
                    sp.dma_start(dst, src).then_inc(vec_loaded, 16)
            sp.dma_start(mask_raw, mask_src).then_inc(mask_loaded, 16)
            if not first:
                sp.dma_start(mask_all, mask_src.partition_broadcast(P)).then_inc(mask_loaded, 16)
            for u in (3, 2) if first else (2, 3):
                sp.wait_ge(w_low if first else w_turned, last_op_of[u - 2] + 1)
                load_raw(u)
            if not first:
                sp.wait_ge(source_stored[0], source_stored[1])
            sp.wait_ge(mask_made, 1)
            sp.dma_start(mask_rows, mask_tile).then_inc(mask_stored, 16)
            sp.wait_ge(mask_stored, 16)
            sp.wait_ge(const_made, CONSTS)

            def iteration(p, a, prev):
                if a is not None:
                    at_least(sp, norm_turned if first else stored, a if first else 16 * a)
                    sp.dma_start(rows[:, :, :], res_view[a]).then_inc(rows_loaded, 16)
                if first and prev is not None:
                    sp.wait_ge(nT_done, prev + 1)
                    sp.dma_start(result[prev], nT[:, :, :]).then_inc(stored, 16)
                if p is not None and not (isinstance(p, int) and p == B - 1):
                    sp.wait_ge(item_done, ITEMS * p + NT)
                    load_tokens(sp, p + 1)
                if a is not None:
                    for half in range(HALVES):
                        sp.wait_ge(shift_copied, HALVES * a + half + 1)
                        for part in range(2):
                            sp.dma_start(
                                f32(stack[SHIFT_ROW + part:SHIFT_ROW + part + 1,
                                          HALF * half:HALF * (half + 1), Q_COLS]),
                                shiftT[HALF * part:HALF * (part + 1), half:half + 1, :],
                            ).then_inc(shift_loaded[half], 16)
                if p is None and load_ahead is not None:
                    for half in range(HALVES):
                        sp.wait_ge(stack_loaded[half], 16 * STACK_DMAS * B)
                    sp.wait_ge(stored, 16 * 2)
                    load_ahead(sp)
                if p is not None:
                    for half in range(HALVES):
                        if a is None:
                            sp.wait_ge(low_done, ITEMS * p + NT + NK + half + 1 if first
                                       else ITEMS * p + NT + GROUPS * (half + 1))
                        else:
                            sp.wait_ge(shifted_done, PSTEPS * a + PSTEPS // HALVES * (half + 1))
                        load_stacks(sp, p, half)
                if a is not None and not first:
                    sp.wait_ge(rows_done, a + 1)
                    sp.dma_start(out_view[a], rows[:, :, :]).then_inc(stored, 16)

            iteration(0, None, None)
            iteration(1, 0, None)
            with sp.Fori(2, B - 1) as i:
                iteration(i, i - 1, i - 2)
            iteration(B - 1, B - 2, B - 3)
            iteration(None, B - 1, B - 2)
            if first:
                sp.wait_ge(nT_done, B)
                sp.dma_start(result[B - 1], nT[:, :, :]).then_inc(stored, 16)
            else:
                sp.wait_ge(stored, 16 * B)

        @block.gpsimd
        def _(pool):
            if first:
                make_identity(pool, ident, ident_made)
                pool.wait_ge(ident_made, 2)
            pool.memset(spread[:, :, :], 0.0).then_inc(const_made, 1)
            pool.wait_ge(const_made, 1)
            pool.affine_select(out=spread[:, :, :].rearrange("p g (j d) -> p g j d", j=HG),
                               in_=spread[:, :, :].rearrange("p g (j d) -> p g j d", j=HG),
                               compare_op=ALU.not_equal, fill=1.0, base=-INV_ROW,
                               pattern=[[-HG, GROUPS], [-1, HG], [0, DH]], channel_multiplier=1).then_inc(const_made, 1)
            pool.wait_ge(const_made, 2)
            pool.memset(half_power[:, :], -0.5).then_inc(const_made, 1)
            pool.wait_ge(const_made, 3)
            pool.memset(eps[:, :], RMS_EPS if first else LN_EPS).then_inc(const_made, 1)
            def ln_rstd(b):
                pool.wait_ge(stats_done, b + 1)
                for t in range(QT):
                    pool.tensor_tensor(stat[:, t, 1:2], stat[:, t, 1:2], eps[:, 0:1], ALU.add).then_inc(rstd_step, 1)
                pool.wait_ge(rstd_step, QT * (b + 1))
                for t in range(QT):
                    n = pool.tensor_tensor(stat[:, t, 2:3], stat[:, t, 1:2], half_power[:, 0:1], ALU.pow)
                n.then_inc(ln_rstd_done, 1)
                pool.wait_ge(ln_step, 2 * (b + 1))
                for t in range(QT):
                    n = pool.tensor_tensor(tokens[:, QT + t, :], tokens[:, QT + t, :], gamma[:, :], ALU.mult)
                n.then_inc(ln_scaled, 1)
                pool.wait_ge(ln_scaled, b + 1)
                for t in range(QT):
                    n = pool.tensor_tensor(tokens[:, QT + t, :], tokens[:, QT + t, :], beta[:, :], ALU.add)
                n.then_inc(ln_done, 1)

            def iteration(p, a):
                if first and a is not None:
                    pool.wait_ge(rows_loaded, 16 * (a + 1))
                    for t in range(QT):
                        n = pool.tensor_tensor(rows[:, t, :], rows[:, t, :], bo[:, :], ALU.add)
                    n.then_inc(rows_biased, 1)
                    pool.wait_ge(mean_sq_done, a + 1)
                    pool.tensor_tensor(stat[:, :, 1], stat[:, :, 0], eps[:, :], ALU.add).then_inc(rstd_step, 1)
                    pool.wait_ge(rstd_step, a + 1)
                    for t in range(QT):
                        n = pool.tensor_tensor(stat[:, t, 2:3], stat[:, t, 1:2], half_power[:, 0:1], ALU.pow)
                    n.then_inc(rstd_done, 1)
                if not first and p is not None and not (isinstance(p, int) and p == B - 1):
                    ln_rstd(p + 1)

            pool.wait_ge(const_made, CONSTS - 1)
            pool.wait_ge(vec_loaded, 16 * VECTORS)
            if not first:
                ln_rstd(0)
                pool.wait_ge(ln_done, 1)
            pool.memset(f32(stack[MASK_ROW:ROWS_ALL, :, :]), 1.0).then_inc(const_made, 1)
            pool.wait_ge(const_made, CONSTS)
            iteration(0, None)
            with pool.Fori(1, B - 1) as i:
                iteration(i, i - 1)
            iteration(B - 1, B - 2)
            iteration(None, B - 1)

        @block.scalar
        def _(act):
            def split_high(n):
                u, src, (high, _low), scale = split_ops[n]
                if first:
                    act.wait_ge(raw_loaded[u % 2], 16 * (u // 2 + 1))
                else:
                    act.wait_ge(w_turned, n + 1)
                act.activation(high, src, ACT.Copy, scale=scale).then_inc(w_high, 1)

            def vectors_ready():
                act.wait_ge(vec_loaded, 16 * VECTORS)
                if first:
                    act.wait_ge(setup_step, 1)
                else:
                    act.activation(tanh_gate[:, :], gate[:, :], ACT.Tanh).then_inc(setup_step, 1)

            def high(b, k):
                act.wait_ge(item_done, ITEMS * b + k + 1)
                ps, done = item_ps[k % 2], ITEMS * b + k + 1
                if k < NT:
                    if not isinstance(b, int) or b > 0:
                        if k < FB - 1:
                            act.wait_ge(v_shared, (FB - 1) * (b - 1) + k + 1)
                        else:
                            act.wait_ge(v_done, KB * b)
                    n = act.activation(hT[0][:, k, :], ps[:, :], ACT.Copy)
                elif not first:
                    g = k - NT
                    at_least(act, stack_loaded[g // GROUPS], 16 * STACK_DMAS * b)
                    n = act.activation(qk[:, g, :].rearrange("p (n s) -> p n s", s=S)[:, 0:4:3, :],
                                       ps[:, :].rearrange("p (n s) -> p n s", s=S), ACT.Copy)
                elif k < NT + NK:
                    g = k - NT
                    at_least(act, stack_loaded[g // GROUPS], 16 * STACK_DMAS * b)
                    n = act.activation(qk[:, g, K_HIGH], ps[:, 0:KEYS], ACT.Identity, bias=bk[:, g:g + 1])
                else:
                    for i in range(2):
                        g = 2 * (k - NT - NK) + i
                        n = act.activation(qk[:, g, Q_HIGH], ps[:, S * i:S * (i + 1)], ACT.Identity, bias=bq[:, g:g + 1])
                n.then_inc(high_done, 1)

            def step_sum(a, k):
                act.wait_ge(max_done, STEPS * a + k + 1)
                for q in ([k % QT] if first else range(QT)):
                    h = k // QT if first else k
                    e = score_ps[:, k % RING, :] if first else score_ps[:, k % RING, S * q:S * (q + 1)]
                    m = act.activation(e, e, ACT.Exp, bias=neg_max[:, q, h:h + 1], accum_out=row_sum[:, q, h:h + 1])
                m.then_inc(sum_done, 1)

            def copy_shift(a, half):
                act.wait_ge(shift_turned, HALVES * a + half + 1)
                at_least(act, shift_loaded[half], 32 * a)
                act.activation(shiftT[:, half, :], o_ps[half][0:SHIFT_ROWS, 0:S], ACT.Copy).then_inc(shift_copied, 1)

            def copy_inv(a, half):
                act.wait_ge(spread_done, HALVES * a + half + 1)
                at_least(act, o_norm_done, FB * a)
                if first and half == 0:
                    at_least(act, stored, 16 * a)
                act.activation(inv_sum[:, GROUPS * half:GROUPS * (half + 1), :].rearrange("p g s -> p (g s)"),
                               o_ps[half][:, :], ACT.Copy).then_inc(inv_copied, 1)

            def exps(a, s):
                act.wait_ge(shifted_done, PSTEPS * a + s + 1)
                if s >= PROBS:
                    act.wait_ge(pv_done, PSTEPS * a + s - PROBS + 1)
                act.activation(probs[:, s % PROBS, :].rearrange("p (a b) -> p a b", a=2),
                               score_ps[:, 2 * (s % 2):2 * (s % 2) + 2, :], ACT.Exp).then_inc(probs_ready, 1)

            def o_high(a, g):
                act.wait_ge(o_norm_done, FB * a + g + 1)
                at_least(act, out_done, a)
                if first:
                    n = act.activation(oT[0][:, g, :], o_norm[:, g % 2, :], ACT.Identity, bias=bv[:, g:g + 1])
                else:
                    n = act.activation(oT[0][:, g, :], o_norm[:, g % 2, :], ACT.Copy)
                n.then_inc(o_high_done, 1)

            def copy_v(b, t):
                act.wait_ge(v_done, KB * b + t + 1)
                at_least(act, pv_done, PSTEPS * b)
                act.activation(v[:, t, :], v_bank(t), ACT.Copy).then_inc(v_copied, 1)

            def iteration(p, a):
                for slot in range(SLOTS + 1):
                    kind, n = kind_of(slot - 1, p, a)
                    if kind == "v":
                        copy_v(a, n)
                    elif kind == "item" and n >= NT:
                        high(p, n)
                    kind, n = kind_of(slot, p, a)
                    if kind == "item" and n < NT:
                        high(p, n)
                    if a is not None:
                        for half in range(HALVES):
                            if TURN_SLOT[half] == slot - 1:
                                copy_shift(a, half)
                        if SPREAD_SLOT == slot - 1:
                            copy_inv(a, 0)
                        if first and slot == AFTER_T:
                            for t in range(PLAIN_V, KB):
                                copy_v(a, t)
                        if 0 < slot <= AFTER_T and sums_later(slot - 1):
                            for k in steps_of(slot - 1, a):
                                step_sum(a, k)
                        if slot < SLOTS and not sums_later(slot):
                            for k in steps_of(slot, a):
                                step_sum(a, k)
                if a is not None:
                    for s in range(PSTEPS):
                        exps(a, s)
                        if s == 1:
                            copy_inv(a, 1)
                        if s >= KB and s % KB == 1:
                            o_high(a, s // KB - 1)
                    o_high(a, FB - 1)

            for kind, n in FIRST:
                if kind == "split":
                    split_high(n)
                else:
                    if n == NT:
                        vectors_ready()
                    high(0, n)
            iteration(1, 0)
            with act.Fori(2, B) as i:
                iteration(i, i - 1)
            iteration(None, B - 1)

        @block.vector
        def _(dve):
            def make_mask():
                dve.wait_ge(mask_loaded, 16 if first else 32)
                if first:
                    dve.memset(mask_tile[:, 0:S], 0.0)
                    dve.tensor_scalar(mask_tile[:, S:2 * S], mask_raw, 0.0, MASKED, ALU.is_equal, ALU.mult
                                      ).then_inc(mask_made, 1)
                else:
                    dve.tensor_scalar(mask_tile, mask_raw, 0.0, MASKED, ALU.is_equal, ALU.mult
                                      ).then_inc(mask_made, 1)

            def split_low(n):
                _u, src, (high, low), scale = split_ops[n]
                dve.wait_ge(w_high, n + 1)
                dve.scalar_tensor_tensor(low, src, scale, f32(high), ALU.mult, ALU.subtract).then_inc(w_low, 1)

            def vectors_ready():
                dve.wait_ge(vec_loaded, 16 * VECTORS)
                if first:
                    dve.tensor_scalar(bq[:, :], bq[:, :], SCALE, None, ALU.mult).then_inc(setup_step, 1)
                    dve.wait_ge(setup_step, 1)
                    return
                dve.tensor_reduce(any_key[:, :], mask_all, AXIS_X, ALU.max).then_inc(part_done, 1)
                dve.wait_ge(part_done, 1)
                dve.tensor_scalar(any_key[:, :], any_key[:, :], 0.0, None, ALU.is_gt).then_inc(part_done, 1)
                dve.wait_ge(part_done, 2)
                dve.reciprocal(any_inv[:, :], any_key[:, :]).then_inc(part_done, 1)
                dve.wait_ge(part_done, 3)
                dve.wait_ge(setup_step, 1)
                dve.scalar_tensor_tensor(gate_b[:, :], any_key[:, :], tanh_gate[:, 0:1], any_inv[:, :],
                                         ALU.mult, ALU.mult).then_inc(part_done, 1)
                dve.wait_ge(part_done, 4)

            def layer_norm_stats(b):
                dve.wait_ge(tokens_loaded, 32 * (b + 1))
                for t in range(QT):
                    n = dve.bn_stats(ln_stats[:, t, :], tokens[:, QT + t, :])
                n.then_inc(ln_step, 1)
                dve.wait_ge(ln_step, 2 * b + 1)
                dve.memset(stat[:, :, 3:4], 0.0)
                for t in range(QT):
                    n = dve.bn_aggr(stat[:, t, 0:2], ln_stats[:, t, :])
                n.then_inc(stats_done, 1)

            def layer_norm(b):
                dve.wait_ge(ln_rstd_done, b + 1)
                for t in range(QT):
                    n = dve.tensor_scalar(tokens[:, QT + t, :], tokens[:, QT + t, :], stat[:, t, 0:1],
                                          stat[:, t, 2:3], ALU.subtract, ALU.mult)
                n.then_inc(ln_step, 1)

            def low(b, k):
                dve.wait_ge(high_done, ITEMS * b + k + 1)
                ps = item_ps[k % 2]
                if k < NT:
                    n = dve.tensor_tensor(hT[1][:, k, :], ps[:, :], f32(hT[0][:, k, :]), ALU.subtract)
                elif not first:
                    g = k - NT
                    dve.tensor_tensor(qk[:, g, Q_LOW], ps[:, 0:S], f32(qk[:, g, Q_HIGH]), ALU.subtract)
                    n = dve.tensor_tensor(qk[:, g, K_LOW], ps[:, S:2 * S], f32(qk[:, g, K_HIGH]), ALU.subtract)
                elif k < NT + NK:
                    g = k - NT
                    n = dve.scalar_tensor_tensor(qk[:, g, K_LOW], ps[:, 0:KEYS], bk[:, g:g + 1],
                                                 f32(qk[:, g, K_HIGH]), ALU.add, ALU.subtract)
                else:
                    for i in range(2):
                        g = 2 * (k - NT - NK) + i
                        n = dve.scalar_tensor_tensor(qk[:, g, Q_LOW], ps[:, S * i:S * (i + 1)], bq[:, g:g + 1],
                                                     f32(qk[:, g, Q_HIGH]), ALU.add, ALU.subtract)
                n.then_inc(low_done, 1)

            def step_max(a, k):
                dve.wait_ge(scores_done, STEPS * a + k + 1)
                bank = score_ps[:, k % RING, :]
                if first:
                    out = neg_max[:, k % QT, k // QT:k // QT + 1]
                else:
                    bank = bank.rearrange("p (q n) -> p q n", q=QT)
                    out = neg_max[:, :, k]
                dve.tensor_reduce(out, bank, AXIS_X, ALU.max, negate=True).then_inc(max_done, 1)

            def make_shift(a, half):
                dve.wait_ge(sum_done, STEPS * a + STEPS // HALVES * (half + 1))
                heads = slice(HALF * half, HALF * (half + 1))
                src, high = neg_max[:, :, heads], shift[:, half, :, 0:HALF]
                dve.tensor_copy(high.bitcast(F32R), src).then_inc(shift_step, 1)
                dve.reciprocal(shift[:, half, :, INV_ROW:SHIFT_ROWS], row_sum[:, :, heads])
                dve.wait_ge(shift_step, HALVES * a + half + 1)
                dve.tensor_tensor(shift[:, half, :, HALF:2 * HALF].bitcast(F32R), src, high, ALU.subtract
                                  ).then_inc(shift_made, 1)

            def normalise(a, g):
                dve.wait_ge(pv_done, PSTEPS * a + KB * (g + 1))
                dve.tensor_tensor(o_norm[:, g % 2, :], o_ps[g % 2][:, 0:S], inv_sum[:, g, :], ALU.mult
                                  ).then_inc(o_norm_done, 1)

            def o_low(a, g):
                dve.wait_ge(o_high_done, FB * a + g + 1)
                if first:
                    n = dve.scalar_tensor_tensor(oT[1][:, g, :], o_norm[:, g % 2, :], bv[:, g:g + 1],
                                                 f32(oT[0][:, g, :]), ALU.add, ALU.subtract)
                else:
                    n = dve.tensor_tensor(oT[1][:, g, :], o_norm[:, g % 2, :], f32(oT[0][:, g, :]), ALU.subtract)
                n.then_inc(o_low_done, 1)

            def finish(a):
                dve.wait_ge(out_done, a + 1)
                if not first:
                    dve.wait_ge(rows_loaded, 16 * (a + 1))
                    for t in range(QT):
                        n = dve.scalar_tensor_tensor(rows[:, t, :], item_ps[t][:, :], gate_b[:, bass.ds(a, 1)],
                                                     rows[:, t, :], ALU.mult, ALU.add)
                    n.then_inc(rows_done, 1)
                    return
                dve.wait_ge(rows_biased, a + 1)
                for t in range(QT):
                    n = dve.tensor_tensor(rows[:, t, :], item_ps[t][:, :], rows[:, t, :], ALU.add)
                n.then_inc(rows_done, 1)

            def square_rows(b):
                dve.wait_ge(rows_done, b + 1)
                at_least(dve, stored, 16 * b)
                for t in range(QT):
                    n = dve.tensor_tensor_reduce(out=squares[:, t, :], in0=rows[:, t, :], in1=rows[:, t, :], scale=1.0 / D,
                                                 scalar=0.0, op0=ALU.mult, op1=ALU.add,
                                                 accum_out=stat[:, t, 0:1])
                n.then_inc(mean_sq_done, 1)

            def scale_rows(b):
                dve.wait_ge(rstd_done, b + 1)
                for t in range(QT):
                    n = dve.tensor_scalar(rows[:, t, :], rows[:, t, :], stat[:, t, 2:3], None, ALU.mult)
                n.then_inc(norm_done, 1)

            def weigh_norm(b):
                dve.wait_ge(norm_turned, b + 1)
                for f in range(FB):
                    n = dve.tensor_scalar(nT[:, f, :], o_ps[f // 2][:, S * (f % 2):S * (f % 2 + 1)],
                                          post_w[:, f:f + 1], None, ALU.mult)
                n.then_inc(nT_done, 1)

            def iteration(p, a, prev):
                for slot in range(SLOTS + 1):
                    steps = steps_of(slot, a) if a is not None and slot < SLOTS else []
                    kind, n = kind_of(slot, p, a)
                    if kind == "item" and n < NT:
                        low(p, n)
                    for k in steps[:1]:
                        step_max(a, k)
                    for half in range(HALVES):
                        if a is not None and TURN_SLOT[half] == slot:
                            make_shift(a, half)
                    kind, n = kind_of(slot - 1, p, a)
                    if kind == "item" and n >= NT:
                        low(p, n)
                    if not first and a is not None and slot == AFTER_T:
                        for t in range(KB):
                            dve.wait_ge(v_done, KB * a + t + 1)
                            at_least(dve, pv_done, PSTEPS * a)
                            dve.tensor_copy(v[:, t, :], v_bank(t)).then_inc(v_copied, 1)
                    for k in steps[1:]:
                        step_max(a, k)
                    if first and prev is not None:
                        if slot == SQUARE_SLOT:
                            square_rows(prev)
                        if slot == SCALE_SLOT:
                            scale_rows(prev)
                        if slot == NORM_SLOT + 1:
                            weigh_norm(prev)
                    if not first and p is not None and not (isinstance(p, int) and p == B - 1) and slot == SLOTS - 1:
                        layer_norm_stats(p + 1)
                if not first and p is not None and not (isinstance(p, int) and p == B - 1):
                    layer_norm(p + 1)
                if a is not None:
                    for g in range(FB):
                        normalise(a, g)
                        o_low(a, g)
                    finish(a)

            for kind, n in FIRST:
                if not first and (kind, n) == ("split", 0):
                    layer_norm_stats(0)
                if not first and (kind, n) == ("split", 2):
                    layer_norm(0)
                if not first and (kind, n) == ("split", FB):
                    make_mask()
                if not first and (kind, n) == ("item", NT + 2):
                    layer_norm_stats(1)
                if not first and (kind, n) == ("item", NT + 3):
                    layer_norm(1)
                if kind == "split":
                    split_low(n)
                else:
                    if n == NT:
                        if first:
                            make_mask()
                        vectors_ready()
                    low(0, n)
            iteration(1, 0, None)
            with dve.Fori(2, B - 1) as i:
                iteration(i, i - 1, i - 2)
            iteration(B - 1, B - 2, B - 3)
            iteration(None, B - 1, B - 2)
            if first:
                square_rows(B - 1)
                scale_rows(B - 1)
                weigh_norm(B - 1)

        @block.tensor
        def _(pe):
            pe.wait_ge(ident_made, 2)

            def turn_weights(n):
                u, ps, _parts, _scale = split_ops[n]
                pe.wait_ge(raw_loaded[u % 2], 16 * (u // 2 + 1))
                if n >= RING:
                    pe.wait_ge(w_low, n - RING + 1)
                for o in range(FB):
                    m = pe.transpose(ps[:, P * o:P * (o + 1)], raw_view(u)[:, o, P * (n % FB):P * (n % FB + 1)],
                                     ident[:, :])
                m.then_inc(w_turned, 1)

            def item(b, a, k, step=None):
                ps = item_ps[k % 2]
                if k < 2 and a is not None:
                    at_least(pe, rows_done, a)
                    if PLAIN_V:
                        pe.wait_ge(v_copied, KB * a + k + 1)
                at_least(pe, low_done, ITEMS * b + k - 1)
                if k < NT:
                    if k == 0:
                        if first:
                            pe.wait_ge(tokens_loaded, 32 * (b + 1))
                        else:
                            pe.wait_ge(ln_done, b + 1)
                            pe.wait_ge(tokens_loaded, 32 * (b + 1))
                    for t in range(2 * QT):
                        n = pe.transpose(ps[:, P * t:P * (t + 1)], tokens[:, t, P * k:P * (k + 1)], ident[:, :])
                else:
                    g = k - NT
                    if not first:
                        parts = [(wq, g), (wk, g)]
                    elif g < NK:
                        parts = [(wk, g)]
                    else:
                        parts = [(wq, 2 * (g - NK)), (wq, 2 * (g - NK) + 1)]
                    width = 2 * S // len(parts)
                    for i, (weight, o) in enumerate(parts):
                        cols = slice(KEY_COL, KEY_COL + KEYS) if weight is wk else slice(0, S)
                        for f in range(FB):
                            if step is not None and (FB * i + f) % len(parts) == 0:
                                step()
                            if g == 0 and i == 0:
                                pe.wait_ge(low_done, ITEMS * b + f + 1)
                            n = product(pe, ps[:, width * i:width * (i + 1)],
                                        [w[:, f, P * o:P * (o + 1)] for w in weight],
                                        [h[:, f, cols] for h in hT], f == 0, f == FB - 1)
                n.then_inc(item_done, 1)

            def v_passes(b, t, f):
                col = KEY_COL + P * t
                return product(pe, v_bank(t), [h[:, f, col:col + P] for h in hT],
                               [w[:, f, :] for w in wv], f == 0, f == FB - 1)

            def v_item(b, t, step):
                at_least(pe, rows_done, b)
                pe.wait_ge(low_done, ITEMS * (b + 1))
                for f in range(FB):
                    step()
                    n = v_passes(b, t, f)
                n.then_inc(v_done, 1)

            def v_share(b, f):
                if f == 0:
                    pe.wait_ge(low_done, ITEMS * (b + 1))
                    at_least(pe, o_norm_done, FB * b)
                for t in range(PLAIN_V, KB):
                    n = v_passes(b, t, f)
                    if f == FB - 1:
                        n.then_inc(v_done, 1)
                if f < FB - 1:
                    n.then_inc(v_shared, 1)

            def scores(a, k):
                if k < RING:
                    at_least(pe, probs_ready, PSTEPS * a)
                    if not first and isinstance(a, int) and a == 0:
                        pe.wait_ge(w_low, SPLITS)
                else:
                    pe.wait_ge(sum_done, STEPS * a + k - RING + 1)
                h = k // QT if first else k
                if h % HALF == 0:
                    pe.wait_ge(stack_loaded[h // HALF], 16 * STACK_DMAS * (a + 1))
                for q in ([k % QT] if first else range(QT)):
                    out = score_ps[:, k % RING, :] if first else score_ps[:, k % RING, S * q:S * (q + 1)]
                    m = pe.matmul(out, stack[0:ROWS_MAX, h, P * q:P * (q + 1)], stack[0:ROWS_MAX, h, K_COLS],
                                  start=True, stop=True)
                m.then_inc(scores_done, 1)

            def turn_shift(a, half):
                pe.wait_ge(shift_made, HALVES * a + half + 1)
                pe.wait_ge(v_copied, KB * (a + 1))
                if first:
                    at_least(pe, nT_done, a)
                at_least(pe, o_norm_done, FB * a)
                for q in range(QT):
                    n = pe.transpose(o_ps[half][0:SHIFT_ROWS, P * q:P * (q + 1)], shift[:, half, q, :], ident[:, :])
                n.then_inc(shift_turned, 1)

            def spread_sums(a, half):
                pe.wait_ge(shift_copied, HALVES * a + half + 1)
                for g in range(GROUPS):
                    n = pe.matmul(o_ps[half][:, S * g:S * (g + 1)], spread[:, g, :], shiftT[:, half, :],
                                  start=True, stop=True)
                n.then_inc(spread_done, 1)

            def shifted(a, s):
                g, kb = s // KB, s % KB
                if s % (2 * KB) == 0:
                    pe.wait_ge(shift_loaded[s // (2 * KB)], 32 * (a + 1))
                if s < 2:
                    pe.wait_ge(sum_done, STEPS * (a + 1) - 2 + 2 * s)
                else:
                    pe.wait_ge(probs_ready, PSTEPS * a + s - 1)
                for j in range(HG):
                    h = HG * g + j
                    n = pe.matmul(score_ps[:, 2 * (s % 2) + j // 2, S * (j % 2):S * (j % 2 + 1)],
                                  stack[0:ROWS_ALL, h, S + P * kb:S + P * (kb + 1)], stack[0:ROWS_ALL, h, Q_COLS],
                                  start=True, stop=True)
                n.then_inc(shifted_done, 1)

            def weigh(a, s):
                g, kb = s // KB, s % KB
                pe.wait_ge(probs_ready, PSTEPS * a + s + 1)
                if kb == 0 and g < 2:
                    pe.wait_ge(inv_copied, HALVES * a + g + 1)
                if kb == 0 and g >= 2:
                    pe.wait_ge(o_norm_done, FB * a + g - 1)
                for j in range(HG):
                    h, to = HG * g + j, slice(DH * j, DH * (j + 1))
                    n = pe.matmul(o_ps[g % 2][to, 0:S], v[:, kb, DH * h:DH * (h + 1)],
                                  probs[:, s % PROBS, S * j:S * (j + 1)], start=(kb == 0), stop=(kb == KB - 1),
                                  skip_group_check=True, tile_position=(0, DH * j))
                n.then_inc(pv_done, 1)

            def project(a, g):
                if isinstance(a, int) and a == 0 and g == 0:
                    pe.wait_ge(w_low, SPLITS)
                pe.wait_ge(o_low_done, FB * a + g + 1)
                for t in range(QT):
                    n = product(pe, item_ps[t][:, :], [o[:, g, P * t:P * (t + 1)] for o in oT],
                                [w[:, g, :] for w in wo], g == 0, g == FB - 1)
                if g == FB - 1:
                    n.then_inc(out_done, 1)

            def turn_norm(a, last=False):
                pe.wait_ge(norm_done, a + 1)
                if not last:
                    pe.wait_ge(v_copied, KB * (a + 2))
                for f in range(FB):
                    for t in range(QT):
                        n = pe.transpose(o_ps[f // 2][:, S * (f % 2) + P * t:S * (f % 2) + P * (t + 1)],
                                         rows[:, t, P * f:P * (f + 1)], ident[:, :])
                n.then_inc(norm_turned, 1)

            def iteration(p, a, prev):
                for slot in range(SLOTS):
                    steps = iter(steps_of(slot, a) if a is not None else [])

                    def step():
                        k = next(steps, None)
                        if k is not None:
                            scores(a, k)

                    kind, n = kind_of(slot, p, a)
                    if kind == "v":
                        v_item(a, n, step)
                    elif kind == "item":
                        item(p, a, n, step)
                    if a is not None and SLOT[slot][0] == "share":
                        v_share(a, 0)
                        v_share(a, 1)
                    for k in steps:
                        scores(a, k)
                    if a is not None and SLOT[slot][0] == "item" and 1 <= n < FB - 1:
                        v_share(a, n + 1)
                    if first and prev is not None and slot == NORM_SLOT:
                        turn_norm(prev)
                    for half in range(HALVES):
                        if a is not None and TURN_SLOT[half] == slot:
                            turn_shift(a, half)
                    if a is not None and SPREAD_SLOT == slot:
                        spread_sums(a, 0)
                if a is not None:
                    shifted(a, 0)
                    shifted(a, 1)
                    spread_sums(a, 1)
                    if p is not None:
                        pe.wait_ge(low_done, ITEMS * (p + 1))
                    else:
                        pe.wait_ge(v_copied, KB * (a + 1))
                    for s in range(PSTEPS):
                        if s + 2 < PSTEPS:
                            shifted(a, s + 2)
                        weigh(a, s)
                        if s >= KB and s % KB == KB - 1 and s < PSTEPS - 1:
                            project(a, s // KB - 1)
                    for g in range(FB - 2, FB):
                        project(a, g)

            for kind, n in FIRST:
                if kind == "item":
                    if n == NT:
                        pe.wait_ge(w_low, SPLITS_OF_K)
                    if n == NT + NK:
                        pe.wait_ge(w_low, SPLITS_OF_Q)
                    item(0, None, n)
                elif not first:
                    turn_weights(n)
            pe.wait_ge(w_low, SPLITS_OF_V)
            pe.wait_ge(const_made, CONSTS)
            iteration(1, 0, None)
            with pe.Fori(2, B) as i:
                iteration(i, i - 1, i - 2)
            iteration(None, B - 1, B - 2)
            if first:
                turn_norm(B - 1, last=True)


def mlp_first_loads(room, given, nT, w1, w2):
    def load(sp):
        w1_view = w1.rearrange("(f p) n -> p f n", p=P)[:, :, 0:CHUNK]
        w2_view = w2.rearrange("(m p) n -> p m n", p=P)[:, 0:FB, :]
        norm = room[:, 1, :].rearrange("p (f s) -> p f s", f=FB)
        sp.dma_start(room[:, 0, :].rearrange("p (f n) -> p f n", f=FB), w1_view).then_inc(given["raw_loaded0"], 16)
        for e in range(CHUNK // S):
            sp.dma_start(norm[:, :, S * e:S * (e + 1)], nT[e]).then_inc(given["norm_loaded"], 16)
        sp.dma_start(room[:, 2, :].rearrange("p (m n) -> p m n", m=FB), w2_view).then_inc(given["raw_loaded1"], 16)
    return load


def layer1_first_loads(room, given, x, context, wq, wk):
    def load_weights(sp):
        for n, w in ((0, wq), (1, wk)):
            sp.dma_start(room[:, 2 * n, :].rearrange("p (f n) -> p f n", f=FB), w.rearrange("(f p) n -> p f n", p=P)
                         ).then_inc(given[f"raw_loaded{n}"], 16)

    def load_tokens(sp):
        tokens = room[:, 1, :].rearrange("p (t d) -> p t d", t=2 * QT)
        for n, src in enumerate((x, context)):
            sp.dma_start(tokens[:, QT * n:QT * (n + 1), :], src[0].rearrange("(t p) d -> p t d", p=P)
                         ).then_inc(given["tokens_loaded"], 16)
    return load_weights, load_tokens


def mlp(nc, nT, x, w1, b1, w2, b2, x1, room, rows, given, nT_stored, load_weights_ahead, load_tokens_ahead):
    CHUNKS = B * S // CHUNK
    PAIR = CHUNK // S
    TT = CHUNK // P
    LAG = 2
    HBUF = 3

    x_view = x.rearrange("(c e) (t p) d -> c p (e t) d", e=PAIR, p=P)
    x1_view = x1.rearrange("(c e) (t p) d -> c p (e t) d", e=PAIR, p=P)
    nT_view = nT.rearrange("(c e) p f s -> c e p f s", e=PAIR)

    ctx = ExitStack()
    with ctx:
        def sb(name, shape, dt=F32):
            return ctx.enter_context(nc.sbuf_tensor(f"mlp_{name}", shape, dt))

        def sem(name):
            return given[name] if name in given else ctx.enter_context(nc.semaphore(f"mlp_{name}"))

        w1_sb = [sb(f"w1_{p}", [P, FB, HIDDEN], F32R) for p in "hl"]
        w2_sb = [sb(f"w2_{p}", [P, MB, D], F32R) for p in "hl"]
        norm = room[:, 1, :].rearrange("p (f s) -> p f s", f=FB)
        norm_p = [sb(f"norm_{p}", [P, FB, CHUNK], F32R) for p in "hl"]
        hidden = sb("hidden", [P, HBUF, CHUNK])
        hidden_p = [sb(f"hidden_{p}", [P, HBUF, CHUNK], F32R) for p in "hl"]
        b1_col = sb("b1_col", [P, MB])
        b2_row = sb("b2_row", [P, D])
        hidden_ps = [ctx.enter_context(nc.psum_tensor(f"mlp_hidden_ps{n}", [P, CHUNK], F32)) for n in range(4)]
        sum_ps = [ctx.enter_context(nc.psum_tensor(f"mlp_sum_ps{n}", [P, D], F32)) for n in range(TT)]

        raw_loaded = [sem(f"raw_loaded{n}") for n in range(2)]
        w_high, w_low, vec_loaded = (sem(n) for n in ("w_high", "w_low", "vec_loaded"))
        norm_loaded, norm_high, norm_low = sem("norm_loaded"), sem("norm_high"), sem("norm_low")
        up_done, gelu_done, hidden_low, down_done = (
            sem(n) for n in ("up_done", "gelu_done", "hidden_low", "down_done"))
        rows_loaded, rows_biased, rows_done, stored = (
            sem(n) for n in ("rows_loaded", "rows_biased", "rows_done", "stored"))

        w1_view = w1.rearrange("(f p) (q n) -> q p f n", p=P, n=CHUNK)
        w2_view = w2.rearrange("(q m p) n -> q p m n", m=FB, p=P)
        stage = [room[:, 2 * n, :].rearrange("p (f n) -> p f n", f=FB) for n in range(2)]
        QUARTER = MB // FB
        UNITS = 2 * MB // QUARTER
        unit_src = [(w1_view if u % 2 == 0 else w2_view)[u // 2] for u in range(UNITS)]

        def unit_part(u, part, which):
            if u % 2 == 0:
                return w1_sb[which][:, part, CHUNK * (u // 2):CHUNK * (u // 2 + 1)]
            return w2_sb[which][:, FB * (u // 2) + part, :]

        def units_behind(m):
            if m % QUARTER in (1, 2) and m // QUARTER < FB - 1:
                return [2 * (m // QUARTER) + 1 + m % QUARTER]
            return []

        block = ctx.enter_context(nc.Block())

        @block.sync
        def _(sp):
            def load_unit(u):
                if u >= 2:
                    sp.wait_ge(w_low, FB * (u - 1))
                sp.dma_start(stage[u % 2][:, :, :], unit_src[u]).then_inc(raw_loaded[u % 2], 16)

            def load_norm(c):
                at_least(sp, norm_low, FB * c)
                for e in range(PAIR):
                    sp.dma_start(norm[:, :, S * e:S * (e + 1)], nT_view[c, e]).then_inc(norm_loaded, 16)

            def load_rows(c):
                at_least(sp, stored, 16 * TT * c)
                sp.dma_start(rows[:, :, :], x_view[c]).then_inc(rows_loaded, 16)

            def store(c):
                for t in range(TT):
                    sp.wait_ge(rows_done, TT * c + t + 1)
                    sp.dma_start(x1_view[c, :, t, :], rows[:, t, :]).then_inc(stored, 16)

            with nc.allow_non_contiguous_dma(reason="a per-feature vector, once"):
                sp.dma_start(b1_col[:, :], b1.rearrange("(m p) -> p m", p=P)).then_inc(vec_loaded, 16)
            sp.dma_start(b2_row[:, :], b2.partition_broadcast(P)).then_inc(vec_loaded, 16)
            load_rows(0)
            for u in range(2, UNITS):
                load_unit(u)
            sp.wait_ge(nT_stored, 16 * B)
            with sp.Fori(1, CHUNKS) as c:
                load_norm(c)
                store(c - 1)
                load_rows(c)
            sp.wait_ge(w_low, FB * UNITS)
            load_weights_ahead(sp)
            sp.wait_ge(norm_low, FB * CHUNKS)
            load_tokens_ahead(sp)
            store(CHUNKS - 1)

        @block.gpsimd
        def _(pool):
            pool.wait_ge(vec_loaded, 32)
            with pool.Fori(0, CHUNKS) as c:
                pool.wait_ge(rows_loaded, 16 * c + 16)
                for t in range(TT):
                    pool.tensor_tensor(rows[:, t, :], rows[:, t, :], b2_row[:, :], ALU.add).then_inc(rows_biased, 1)

        @block.scalar
        def _(act):
            def split_high(u):
                act.wait_ge(raw_loaded[u % 2], 16 * (u // 2 + 1))
                for part in range(FB):
                    act.activation(unit_part(u, part, 0), stage[u % 2][:, part, :], ACT.Copy).then_inc(w_high, 1)

            def norm_high_parts(c):
                act.wait_ge(norm_loaded, 16 * PAIR * c + 16 * PAIR)
                at_least(act, up_done, MB * c)
                for f in range(FB):
                    act.activation(norm_p[0][:, f, :], norm[:, f, :], ACT.Copy).then_inc(norm_high, 1)

            def gelu(c, m):
                act.wait_ge(up_done, MB * c + m + 1)
                at_least(act, down_done, MB * c + max(m - HBUF + 1, 0))
                act.activation(hidden[:, m % HBUF, :], hidden_ps[m % 4][:, :], ACT.Gelu_apprx_tanh,
                               bias=b1_col[:, m:m + 1])
                act.activation(hidden_p[0][:, m % HBUF, :], hidden_ps[m % 4][:, :], ACT.Gelu_apprx_tanh,
                               bias=b1_col[:, m:m + 1]).then_inc(gelu_done, 1)

            split_high(0)
            norm_high_parts(0)
            split_high(1)
            act.wait_ge(vec_loaded, 32)
            for m in range(MB):
                gelu(0, m)
                for u in units_behind(m):
                    split_high(u)
            with act.Fori(1, CHUNKS) as c:
                norm_high_parts(c)
                for m in range(MB):
                    gelu(c, m)

        @block.vector
        def _(dve):
            def split_low(u):
                for part in range(FB):
                    dve.wait_ge(w_high, FB * u + part + 1)
                    dve.tensor_tensor(unit_part(u, part, 1), stage[u % 2][:, part, :], f32(unit_part(u, part, 0)),
                                      ALU.subtract).then_inc(w_low, 1)

            def norm_low_parts(c):
                for f in range(FB):
                    dve.wait_ge(norm_high, FB * c + f + 1)
                    dve.tensor_tensor(norm_p[1][:, f, :], norm[:, f, :], f32(norm_p[0][:, f, :]), ALU.subtract
                                      ).then_inc(norm_low, 1)

            def low(c, m):
                dve.wait_ge(gelu_done, MB * c + m + 1)
                dve.tensor_tensor(hidden_p[1][:, m % HBUF, :], hidden[:, m % HBUF, :],
                                  f32(hidden_p[0][:, m % HBUF, :]), ALU.subtract).then_inc(hidden_low, 1)

            def finish(c):
                dve.wait_ge(down_done, MB * c + MB)
                dve.wait_ge(rows_biased, TT * c + TT)
                for t in range(TT):
                    dve.tensor_tensor(rows[:, t, :], sum_ps[t][:, :], rows[:, t, :], ALU.add).then_inc(rows_done, 1)

            split_low(0)
            norm_low_parts(0)
            split_low(1)
            for m in range(MB):
                low(0, m)
                for u in units_behind(m):
                    split_low(u)
            norm_low_parts(1)
            finish(0)
            with dve.Fori(1, CHUNKS - 1) as c:
                for m in range(MB):
                    low(c, m)
                norm_low_parts(c + 1)
                finish(c)
            for m in range(MB):
                low(CHUNKS - 1, m)
            finish(CHUNKS - 1)

        @block.tensor
        def _(pe):
            def up(c, m):
                if m >= 4:
                    pe.wait_ge(gelu_done, MB * c + m - 3)
                for f in range(FB):
                    if isinstance(c, int) and m % QUARTER == 0:
                        pe.wait_ge(w_low, FB * (2 * (m // QUARTER)) + f + 1)
                    if m == 0:
                        pe.wait_ge(norm_low, FB * c + f + 1)
                    n = product(pe, hidden_ps[m % 4][:, :], [w[:, f, P * m:P * (m + 1)] for w in w1_sb],
                                [t[:, f, :] for t in norm_p], f == 0, f == FB - 1)
                n.then_inc(up_done, 1)

            def down(c, m):
                if isinstance(c, int):
                    pe.wait_ge(w_low, FB * (2 * (m // QUARTER) + 1) + m % QUARTER + 1)
                pe.wait_ge(hidden_low, MB * c + m + 1)
                for t in range(TT):
                    if m == 0:
                        at_least(pe, rows_done, TT * c)
                    n = product(pe, sum_ps[t][:, :], [h[:, m % HBUF, P * t:P * (t + 1)] for h in hidden_p],
                                [w[:, m, :] for w in w2_sb], m == 0, m == MB - 1)
                n.then_inc(down_done, 1)

            def chunk(c):
                for m in range(MB + LAG):
                    if m < MB:
                        up(c, m)
                    if m >= LAG:
                        down(c, m - LAG)

            chunk(0)
            with pe.Fori(1, CHUNKS) as c:
                chunk(c)


def build(nc, t, out):
    nT = nc.dram_tensor("norm_transposed", [B, P, FB, S], F32).ap()
    x1 = nc.dram_tensor("layer0_result", [B, S, D], F32).ap()
    mask_rows0 = nc.dram_tensor("mask_rows0", [B, 2 * S], F32).ap()
    mask_rows1 = nc.dram_tensor("mask_rows1", [B, S], F32).ap()
    with ExitStack() as ctx:
        def sem(name):
            return ctx.enter_context(nc.semaphore(name))

        room = ctx.enter_context(nc.sbuf_tensor("room", [P, 3, FB * CHUNK], F32))
        norm_room = ctx.enter_context(nc.sbuf_tensor("norm_room", [P, FB, S], F32))
        ident = ctx.enter_context(nc.sbuf_tensor("ident", [P, P], F32))
        ident_made = sem("ident_made")
        norm_stored, x1_stored = sem("norm_stored"), sem("x1_stored")
        mlp_given = {name: sem(f"mlp_{name}") for name in ("raw_loaded0", "raw_loaded1", "norm_loaded")}
        layer1_given = {name: sem(f"l1_{name}") for name in ("raw_loaded0", "raw_loaded1", "tokens_loaded")}
        layer1_given["ident_made"] = ident_made

        attention_layer(
            nc, 0, t["x"], t["ctx_2048"], t["mask_BxS2_ik0"],
            {"q": t["L0_xattn_q_w"], "kv": t["L0_xattn_kv_w"], "o": t["L0_xattn_out_w"]},
            {"q_b": t["L0_xattn_q_b"], "kv_b": t["L0_xattn_kv_b"], "out_b": t["L0_xattn_out_b"],
             "post_w": t["L0_xattn_postnorm_w"]},
            t["x"], mask_rows0, nT, room, {"stored": norm_stored, "ident_made": ident_made}, norm_room, ident,
            load_ahead=mlp_first_loads(room, mlp_given, nT, t["L0_xattn_mlp_w1"], t["L0_xattn_mlp_w2"]))
        rows = ctx.enter_context(nc.sbuf_tensor("rows", [P, CHUNK // P, D], F32))
        load_weights_ahead, load_tokens_ahead = layer1_first_loads(
            room, layer1_given, x1, t["ctx_2048"], t["L1_xattn_Wq"], t["L1_xattn_Wk"])
        mlp(nc, nT, t["x"], t["L0_xattn_mlp_w1"], t["L0_xattn_mlp_b1"], t["L0_xattn_mlp_w2"],
            t["L0_xattn_mlp_b2"], x1, room, rows, {**mlp_given, "stored": x1_stored}, norm_stored,
            load_weights_ahead, load_tokens_ahead)
        attention_layer(
            nc, 1, x1, t["ctx_2048"], t["mask_BxS2_bf1"],
            {"q": t["L1_xattn_Wq"], "k": t["L1_xattn_Wk"], "v": t["L1_xattn_Wv"], "o": t["L1_xattn_Wo"]},
            {"gamma": t["L1_xattn_ln_gamma"], "beta": t["L1_xattn_ln_beta"], "gate": t["L1_xattn_gate"]},
            x1, mask_rows1, out, room, layer1_given, norm_room, ident,
            source_stored=(x1_stored, 16 * (CHUNK // P) * (B * S // CHUNK)))


INPUTS = ["x", "ctx_2048", "mask_BxS2_ik0", "mask_BxS2_bf1", "L0_xattn_q_w", "L0_xattn_q_b", "L0_xattn_kv_w",
          "L0_xattn_kv_b", "L0_xattn_out_w", "L0_xattn_out_b", "L0_xattn_postnorm_w", "L0_xattn_mlp_w1",
          "L0_xattn_mlp_b1", "L0_xattn_mlp_w2", "L0_xattn_mlp_b2", "L1_xattn_Wq", "L1_xattn_Wk", "L1_xattn_Wv",
          "L1_xattn_Wo", "L1_xattn_ln_gamma", "L1_xattn_ln_beta", "L1_xattn_gate"]


def kernel(**inputs):
    import numpy as np
    import concourse.bacc as bacc
    from concourse.bass_utils import run_bass_kernel_spmd

    nc = bacc.Bacc("TRN2", target_bir_lowering=False, num_devices=1)
    arrays, tensors = {}, {}
    for name in INPUTS:
        a = np.ascontiguousarray(inputs[name])
        if a.dtype == np.bool_:
            a = a.view(np.uint8)
        arrays[f"in_{name}"] = a
        tensors[name] = nc.dram_tensor(f"in_{name}", a.shape, mybir.dt.from_np(a.dtype), kind="ExternalInput").ap()
    out = nc.dram_tensor("out", [B, S, D], F32, kind="ExternalOutput").ap()
    build(nc, tensors, out)
    done = run_bass_kernel_spmd(nc, [arrays], core_ids=[0])
    return done.results[0]["out"]
```
